# Optimizing a Trainium2 kernel written in Bass

```python
import numpy as np
import jax
import jax.numpy as jnp

def _softmax(x, axis=-1):
    return jax.nn.softmax(x, axis=axis)

def _gelu(x):
    return jax.nn.gelu(x, approximate=True)

def _silu(x):
    return jax.nn.silu(x)

def _sigmoid(x):
    return jax.nn.sigmoid(x)

def _layernorm(x, axis=-1, eps=1e-05):
    m = jnp.mean(x, axis=axis, keepdims=True)
    v = jnp.var(x, axis=axis, keepdims=True)
    return (x - m) / jnp.sqrt(v + eps)

def _scatter_add(tgt, idx, src, axis=0):
    return tgt.at[idx].add(src)

def _segment_sum(src, seg, n):
    return jax.ops.segment_sum(src, seg, n)
kernel_name = 'mk_rec_standalone_d1_rec_r8_4386bc'

def setup_inputs(seed: int=0):
    np.random.seed(seed)
    _w = jnp.asarray

    def _rec_inputs():
        import jax
        import jax.numpy as jnp
        _rk = jax.random.key(seed)
        r_dense_x = 8.7408e-05 + 1.0001 * jax.random.normal(jax.random.fold_in(_rk, 1), (2048, 13), jnp.float32)
        r_lS_i = jnp.stack([jax.random.randint(jax.random.fold_in(jax.random.fold_in(_rk, 2), 0), (2048,), 4, 99994, jnp.int32), jax.random.randint(jax.random.fold_in(jax.random.fold_in(_rk, 2), 1), (2048,), 0, 99999, jnp.int32), jax.random.randint(jax.random.fold_in(jax.random.fold_in(_rk, 2), 2), (2048,), 1, 99998, jnp.int32), jax.random.randint(jax.random.fold_in(jax.random.fold_in(_rk, 2), 3), (2048,), 2, 99995, jnp.int32), jax.random.randint(jax.random.fold_in(jax.random.fold_in(_rk, 2), 4), (2048,), 0, 99999, jnp.int32), jax.random.randint(jax.random.fold_in(jax.random.fold_in(_rk, 2), 5), (2048,), 4, 12500, jnp.int32), jax.random.randint(jax.random.fold_in(jax.random.fold_in(_rk, 2), 6), (2048,), 0, 99999, jnp.int32), jax.random.randint(jax.random.fold_in(jax.random.fold_in(_rk, 2), 7), (2048,), 0, 99993, jnp.int32), jax.random.randint(jax.random.fold_in(jax.random.fold_in(_rk, 2), 8), (2048,), 2, 99998, jnp.int32), jax.random.randint(jax.random.fold_in(jax.random.fold_in(_rk, 2), 9), (2048,), 2, 12500, jnp.int32), jax.random.randint(jax.random.fold_in(jax.random.fold_in(_rk, 2), 10), (2048,), 2, 12500, jnp.int32), jax.random.randint(jax.random.fold_in(jax.random.fold_in(_rk, 2), 11), (2048,), 2, 99998, jnp.int32), jax.random.randint(jax.random.fold_in(jax.random.fold_in(_rk, 2), 12), (2048,), 1, 99995, jnp.int32), jax.random.randint(jax.random.fold_in(jax.random.fold_in(_rk, 2), 13), (2048,), 5, 12500, jnp.int32), jax.random.randint(jax.random.fold_in(jax.random.fold_in(_rk, 2), 14), (2048,), 8, 12500, jnp.int32), jax.random.randint(jax.random.fold_in(jax.random.fold_in(_rk, 2), 15), (2048,), 0, 99999, jnp.int32), jax.random.randint(jax.random.fold_in(jax.random.fold_in(_rk, 2), 16), (2048,), 9, 99999, jnp.int32), jax.random.randint(jax.random.fold_in(jax.random.fold_in(_rk, 2), 17), (2048,), 2, 99998, jnp.int32), jax.random.randint(jax.random.fold_in(jax.random.fold_in(_rk, 2), 18), (2048,), 3, 12500, jnp.int32), jax.random.randint(jax.random.fold_in(jax.random.fold_in(_rk, 2), 19), (2048,), 6, 99997, jnp.int32), jax.random.randint(jax.random.fold_in(jax.random.fold_in(_rk, 2), 20), (2048,), 5, 12500, jnp.int32), jax.random.randint(jax.random.fold_in(jax.random.fold_in(_rk, 2), 21), (2048,), 0, 99999, jnp.int32), jax.random.randint(jax.random.fold_in(jax.random.fold_in(_rk, 2), 22), (2048,), 1, 12500, jnp.int32), jax.random.randint(jax.random.fold_in(jax.random.fold_in(_rk, 2), 23), (2048,), 4, 99999, jnp.int32), jax.random.randint(jax.random.fold_in(jax.random.fold_in(_rk, 2), 24), (2048,), 0, 99997, jnp.int32), jax.random.randint(jax.random.fold_in(jax.random.fold_in(_rk, 2), 25), (2048,), 3, 12500, jnp.int32)], axis=0)
        return (r_dense_x, r_lS_i)
    r_dense_x, r_lS_i = _rec_inputs()

    def _L0_rec_setup():
        import jax, jax.numpy as jnp
        import numpy as np
        B = 4096
        M = 128
        N_TAB = 26
        N_ROWS = 12500
        LN_BOT = [13, 512, 256, 128]
        LN_TOP = [479, 1024, 1024, 1]
        _LI, _LJ = np.tril_indices(N_TAB + 1, k=-1)

        def _mlp_params(key, ln):
            ws, bs = ([], [])
            for i in range(len(ln) - 1):
                n, m = (ln[i], ln[i + 1])
                key, k1, k2 = jax.random.split(key, 3)
                ws.append(jax.random.normal(k1, (m, n), jnp.float32) * np.sqrt(2.0 / (m + n)))
                bs.append(jax.random.normal(k2, (m,), jnp.float32) * np.sqrt(1.0 / m))
            return (ws, bs)

        def _forward(dense_x, lS_i, emb_W, bot_w0, bot_b0, bot_w1, bot_b1, bot_w2, bot_b2, top_w0, top_b0, top_w1, top_b1, top_w2, top_b2):
            x = jax.nn.relu(dense_x @ bot_w0.T + bot_b0)
            x = jax.nn.relu(x @ bot_w1.T + bot_b1)
            x = jax.nn.relu(x @ bot_w2.T + bot_b2)
            ly = jax.vmap(lambda W, idx: W[idx])(emb_W, lS_i)
            T = jnp.concatenate([x[:, None, :], jnp.transpose(ly, (1, 0, 2))], axis=1)
            Z = jnp.einsum('bid,bjd->bij', T, T)
            Zflat = Z[:, _LI, _LJ]
            R = jnp.concatenate([x, Zflat], axis=1)
            z = jax.nn.relu(R @ top_w0.T + top_b0)
            z = jax.nn.relu(z @ top_w1.T + top_b1)
            p = jax.nn.sigmoid(z @ top_w2.T + top_b2)
            return p
        key = jax.random.key(seed)
        kd, ki, ke, kb, kt = jax.random.split(key, 5)
        dense_x = jax.random.normal(kd, (B, LN_BOT[0]), jnp.float32)
        lS_i = jax.random.randint(ki, (N_TAB, B), 0, N_ROWS, dtype=jnp.int64)
        lS_o = jnp.tile(jnp.arange(B, dtype=jnp.int64), (N_TAB, 1))
        bound = np.sqrt(1.0 / N_ROWS)
        emb_W = jax.random.uniform(ke, (N_TAB, N_ROWS, M), jnp.float32, -bound, bound)
        bw, bb = _mlp_params(kb, LN_BOT)
        tw, tb = _mlp_params(kt, LN_TOP)
        return {'dense_x': dense_x, 'lS_i': lS_i, 'lS_o': lS_o, 'emb_W': emb_W, 'bot_w0': bw[0], 'bot_b0': bb[0], 'bot_w1': bw[1], 'bot_b1': bb[1], 'bot_w2': bw[2], 'bot_b2': bb[2], 'top_w0': tw[0], 'top_b0': tb[0], 'top_w1': tw[1], 'top_b1': tb[1], 'top_w2': tw[2], 'top_b2': tb[2]}
    _L0_rec_all = _L0_rec_setup()
    _L0_rec_in = {k: v for k, v in _L0_rec_all.items() if k in ('lS_o', 'emb_W', 'bot_w0', 'bot_b0', 'bot_w1', 'bot_b1', 'bot_w2', 'bot_b2', 'top_w0', 'top_b0', 'top_w1', 'top_b1', 'top_w2', 'top_b2')}
    del _L0_rec_all
    return {'r_dense_x': r_dense_x, 'r_lS_i': r_lS_i, 'L0_rec_lS_o': _L0_rec_in['lS_o'], 'L0_rec_emb_W': _L0_rec_in['emb_W'], 'L0_rec_bot_w0': _L0_rec_in['bot_w0'], 'L0_rec_bot_b0': _L0_rec_in['bot_b0'], 'L0_rec_bot_w1': _L0_rec_in['bot_w1'], 'L0_rec_bot_b1': _L0_rec_in['bot_b1'], 'L0_rec_bot_w2': _L0_rec_in['bot_w2'], 'L0_rec_bot_b2': _L0_rec_in['bot_b2'], 'L0_rec_top_w0': _L0_rec_in['top_w0'], 'L0_rec_top_b0': _L0_rec_in['top_b0'], 'L0_rec_top_w1': _L0_rec_in['top_w1'], 'L0_rec_top_b1': _L0_rec_in['top_b1'], 'L0_rec_top_w2': _L0_rec_in['top_w2'], 'L0_rec_top_b2': _L0_rec_in['top_b2']}

def reference(r_dense_x, r_lS_i, L0_rec_lS_o, L0_rec_emb_W, L0_rec_bot_w0, L0_rec_bot_b0, L0_rec_bot_w1, L0_rec_bot_b1, L0_rec_bot_w2, L0_rec_bot_b2, L0_rec_top_w0, L0_rec_top_b0, L0_rec_top_w1, L0_rec_top_b1, L0_rec_top_w2, L0_rec_top_b2):
    import jax
    import jax.numpy as jnp

    def _L0_rec_ref(dense_x, lS_i, lS_o, emb_W, bot_w0, bot_b0, bot_w1, bot_b1, bot_w2, bot_b2, top_w0, top_b0, top_w1, top_b1, top_w2, top_b2):
        import jax, jax.numpy as jnp
        import numpy as np
        B = 4096
        M = 128
        N_TAB = 26
        N_ROWS = 12500
        LN_BOT = [13, 512, 256, 128]
        LN_TOP = [479, 1024, 1024, 1]
        _LI, _LJ = np.tril_indices(N_TAB + 1, k=-1)

        def _mlp_params(key, ln):
            ws, bs = ([], [])
            for i in range(len(ln) - 1):
                n, m = (ln[i], ln[i + 1])
                key, k1, k2 = jax.random.split(key, 3)
                ws.append(jax.random.normal(k1, (m, n), jnp.float32) * np.sqrt(2.0 / (m + n)))
                bs.append(jax.random.normal(k2, (m,), jnp.float32) * np.sqrt(1.0 / m))
            return (ws, bs)

        def _forward(dense_x, lS_i, emb_W, bot_w0, bot_b0, bot_w1, bot_b1, bot_w2, bot_b2, top_w0, top_b0, top_w1, top_b1, top_w2, top_b2):
            x = jax.nn.relu(dense_x @ bot_w0.T + bot_b0)
            x = jax.nn.relu(x @ bot_w1.T + bot_b1)
            x = jax.nn.relu(x @ bot_w2.T + bot_b2)
            ly = jax.vmap(lambda W, idx: W[idx])(emb_W, lS_i)
            T = jnp.concatenate([x[:, None, :], jnp.transpose(ly, (1, 0, 2))], axis=1)
            Z = jnp.einsum('bid,bjd->bij', T, T)
            Zflat = Z[:, _LI, _LJ]
            R = jnp.concatenate([x, Zflat], axis=1)
            z = jax.nn.relu(R @ top_w0.T + top_b0)
            z = jax.nn.relu(z @ top_w1.T + top_b1)
            p = jax.nn.sigmoid(z @ top_w2.T + top_b2)
            return p
        del lS_o
        return _forward(dense_x, lS_i, emb_W, bot_w0, bot_b0, bot_w1, bot_b1, bot_w2, bot_b2, top_w0, top_b0, top_w1, top_b1, top_w2, top_b2)
    y = _L0_rec_ref(r_dense_x, r_lS_i, L0_rec_lS_o, L0_rec_emb_W, L0_rec_bot_w0, L0_rec_bot_b0, L0_rec_bot_w1, L0_rec_bot_b1, L0_rec_bot_w2, L0_rec_bot_b2, L0_rec_top_w0, L0_rec_top_b0, L0_rec_top_w1, L0_rec_top_b1, L0_rec_top_w2, L0_rec_top_b2)
    return y

_drawn_inputs = setup_inputs


def setup_inputs(seed=0):
    import zlib

    import numpy as np

    out = dict(_drawn_inputs(seed))
    spreads = {}
    factors = {'r_dense_x': 8.0,
     'L0_rec_emb_W': 8.0,
     'L0_rec_bot_w0': 8.0,
     'L0_rec_bot_b0': 8.0,
     'L0_rec_bot_w1': 8.0,
     'L0_rec_bot_b1': 8.0,
     'L0_rec_bot_w2': 8.0,
     'L0_rec_bot_b2': 26.322,
     'L0_rec_top_w0': 6.295,
     'L0_rec_top_b0': 64.0,
     'L0_rec_top_w1': 8.0,
     'L0_rec_top_b1': 154.311,
     'L0_rec_top_w2': 7.9}
    for name, (base, spread) in spreads.items():
        noise = np.random.default_rng([zlib.crc32(name.encode()), seed]).standard_normal(out[name].shape)
        drawn = base * np.exp(spread * noise) if base else spread * noise
        out[name] = jnp.asarray(drawn.astype(out[name].dtype))
    for name, factor in factors.items():
        out[name] = (out[name] * factor).astype(out[name].dtype)
    return out
```

```python
import concourse.bass as bass
from concourse import mybir
from contextlib import ExitStack

F32, F32R = mybir.dt.float32, mybir.dt.float32r
I32, U32 = mybir.dt.int32, mybir.dt.uint32
ACT, ALU = mybir.ActivationFunctionType, mybir.AluOpType

P = 128
BATCH, TABLES, ROWS, D = 2048, 26, 12500, 128
DENSE, BOT1, BOT2 = 13, 512, 256
TOP = 1024
TILE = 256
TILES = BATCH // TILE
HALVES = TILE // P
GROUPS = TILE // 4
PITCH = 32
FEATURES = TABLES + 1
M1, M2, MT = BOT1 // P, BOT2 // P, TOP // P
WIDTH = [FEATURES - 1 - 2 * a for a in range(TABLES // 2)]
START = [sum(WIDTH[:a]) for a in range(TABLES // 2)]
HALF_PAIRS = sum(WIDTH)
PAIR_PITCH = 192
UNITS = [(4 * u, min(4, TABLES - 4 * u)) for u in range(7)]
TILE_UNITS = HALVES * len(UNITS)
COL_B0, COL_B1, COL_B2 = 0, M1, M1 + M2
COL_T0 = M1 + M2 + 1
COL_T1, COL_W2 = COL_T0 + MT, COL_T0 + 2 * MT
COL_LAST = COL_T0 + 3 * MT
COLUMNS = COL_LAST + 1
STAGED = 1024
SLOTS = 4

BOTTOM = [("bottom0", 0), ("bottom0", 1), ("bottom1", 0), ("bottom2", 0)]
TOP1_AND_BOTTOM = [
    ("bottom0", 0), ("top1", 0), ("turn", 6), ("bottom0", 1), ("turn", 7), ("top1", 1), ("turn", 8),
    ("bottom1", 0), ("turn", 9), ("top1", 2), ("turn", 10), ("bottom2", 0), ("turn", 11),
    ("top1", 3), ("turn", 12), ("turn", 13)]
DOT = [("dot", n) for n in range(8)]
DOT_AND_LAST = [("dot", 0), ("dot", 1), ("last", 0)] + [("dot", n) for n in range(2, 8)]
TO_TOP0 = [
    ("turn", 0), ("turn", 1), ("turn", 2), ("pairs", 0), ("pairs", 1), ("x part", 0), ("turn", 3),
    ("flat", 0), ("x part", 1), ("top0", 0), ("top0", 1), ("turn", 4), ("top0", 2), ("turn", 5),
    ("top0", 3)]


def uses(steps):
    return [s for s in steps if s[0] not in ("turn", "x part")]


NEEDS = {"bottom1": "bottom0", "bottom2": "bottom1", "flat": "pairs", "top0": "flat", "last": "top1",
         "dot": "bottom2"}
SPLIT = ("bottom0", "bottom1", "top0")


def no_turns(steps):
    return [s for s in steps if s[0] != "turn"]


FIRST = [("turn", n) for n in range(TILE_UNITS)]
PROLOGUE = BOTTOM + FIRST + DOT
LOOP = TOP1_AND_BOTTOM + DOT_AND_LAST
EPILOGUE = [("top1", n) for n in range(4)] + [("last", 0)]
PROLOGUE_USES = len(uses(PROLOGUE + TO_TOP0))
LOOP_USES = len(uses(LOOP + TO_TOP0))
assert LOOP_USES % 3 == 0


def dlrm(nc, indices, tables, dense, bot_w0, bot_w1, bot_w2, top_w0, top_w1, columns, out):
    table_rows = tables.rearrange("t r d -> (t r) d")
    ctx = ExitStack()
    with ctx:
        def sb(name, shape, dt):
            return ctx.enter_context(nc.sbuf_tensor(name, shape, dt))

        def sem(name):
            return ctx.enter_context(nc.semaphore(name))

        z0_at = (nc.sbuf_base + 31) // 32 * 32
        sb("z0_region", [P, 2 * MT * TILE], F32)
        dots_at = (nc.sbuf_base + 31) // 32 * 32
        sb("dots_region", [P, 2 * M1 * TILE], F32)
        staged = nc.alloc_sbuf_tensor_at("staged", [P, SLOTS, STAGED], F32, offset=z0_at)
        z0 = nc.alloc_sbuf_tensor_at("z0", [P, 2, MT, TILE], F32R, offset=z0_at)
        dots = nc.alloc_sbuf_tensor_at("dots", [P, TABLES, GROUPS], F32, offset=dots_at)
        h0 = nc.alloc_sbuf_tensor_at("h0", [P, 2, M1, TILE], F32R, offset=dots_at)

        ring = sb("ring", [P, TABLES, D], F32)
        vecs = sb("vecs", [P, GROUPS, 4, PITCH], F32)
        w_bot0 = sb("w_bot0", [96, BOT1], F32R)
        dense_at = (nc.sbuf_base + 31) // 32 * 32
        sb("dense_region", [P, BATCH], F32)
        dense_hlh = nc.alloc_sbuf_tensor_at("dense_hlh", [96, BATCH], F32R, offset=dense_at)
        probs = nc.alloc_sbuf_tensor_at("probs", [P, BATCH], F32, offset=dense_at)
        w_bot1 = sb("w_bot1", [P, 2, M1, BOT2], F32R)
        w_bot2 = sb("w_bot2", [P, 2, M2, D], F32R)
        w_top0 = sb("w_top0", [P, 2, 4, TOP], F32R)
        w_top1 = sb("w_top1", [P, 2, MT, TOP], F32R)
        x = sb("x", [P, 2, TILE], F32R)
        flat_a = sb("flat_a", [P, 2, 2, TILE], F32R)
        h1 = flat_a
        flat_b = sb("flat_b", [P, 2, TILE], F32R)
        pairs = sb("pairs", [P, 4, PAIR_PITCH], F32)
        relu = sb("relu", [P, 2, TILE], F32)
        z1 = sb("z1", [P, 2, 2, TILE], F32)
        weighted = sb("weighted", [P, TILE], F32)
        rows = sb("rows", [P, TILES * HALVES, TABLES], I32)
        row_now = [sb(f"row_now{h}", [P, TABLES], U32) for h in range(HALVES)]
        cols = sb("cols", [P, COLUMNS], F32)
        ident = sb("ident", [P, P], F32)
        ones = sb("ones", [P, P], F32)
        logit = sb("logit", [1, TILE], F32)
        wrap = z1[:, :, :, :].bitcast(I32).rearrange("p a b n -> p (a b n)")
        base = relu[:, :, :].bitcast(I32).rearrange("p a n -> p (a n)")

        turned = [ctx.enter_context(nc.psum_tensor(f"turned{n}", [P, 4, P], F32)) for n in range(2)]
        banks = [ctx.enter_context(nc.psum_tensor(f"banks{n}", [P, 2, 512], F32)) for n in range(3)]

        idx_in, cols_in = sem("idx_in"), sem("cols_in")
        raw_in = [sem(f"raw_in{n}") for n in range(SLOTS)]
        high_made, low_made = sem("high_made"), sem("low_made")
        const_made = sem("const_made")
        zero_made = sem("zero_made")
        rows_step = sem("rows_step")
        row_ready = [sem(f"row_ready{h}") for h in range(HALVES)]
        gathered = [sem(f"gathered{u}") for u in range(len(UNITS))]
        turns = sem("turns")
        act_kept, dve_kept = sem("act_kept"), sem("dve_kept")
        filled = sem("filled")
        act_done, dve_done = sem("act_done"), sem("dve_done")
        relu_made = sem("relu_made")
        weighted_made = sem("weighted_made")
        sent = sem("sent")

        def pair(n):
            return banks[n % 3]

        RAW = ([("bot0", 96, BOT1)] + [("dense", 96, STAGED)] * 2 + [("bot1", P, M1 * BOT2), ("bot2", P, M2 * D)]
               + [("top0", P, TOP)] * 4 + [("top1", P, TOP)] * MT)
        RAW_DMAS = [3 if rows_ == 96 else 1 for _, rows_, _ in RAW]

        def raw_parts(n):
            kind, nrows, ncols = RAW[n]
            k = n - [r[0] for r in RAW].index(kind)
            slot = staged[0:nrows, n % SLOTS, 0:ncols]
            if kind == "bot0":
                return slot, w_bot0[:, :], None
            if kind == "dense":
                return slot, dense_hlh[:, k * STAGED:(k + 1) * STAGED], None
            if kind == "bot1":
                return slot, *(w_bot1[:, s, :, :].rearrange("p k m -> p (k m)") for s in range(2))
            if kind == "bot2":
                return slot, *(w_bot2[:, s, :, :].rearrange("p k m -> p (k m)") for s in range(2))
            w = w_top0 if kind == "top0" else w_top1
            return slot, w[:, 0, k, :], w[:, 1, k, :]

        def raw_count(n):
            return 16 * sum(RAW_DMAS[n % SLOTS:n + 1:SLOTS])

        def vecs_out(n):
            h, (first, count) = n // len(UNITS), UNITS[n % len(UNITS)]
            return vecs[:, :, 2 * h:2 * h + 2, 1 + first:1 + first + count].rearrange("p g q f -> p f q g")

        def turned_in(n):
            count = UNITS[n % len(UNITS)][1]
            return turned[n % 2][:, 0:count, :].rearrange("p f (q g) -> p f q g", q=2)

        def dots_in(src, q):
            groups = src[32 * q:32 * q + 32, :, :].rearrange("i b (g c) -> i (b g) c", g=4)
            return groups[:, :, q * FEATURES:q * FEATURES + TABLES]

        def dots_out(n, q):
            return dots[32 * q:32 * q + 32, :, 8 * n:8 * n + 8].rearrange("i j g -> i g j")

        def pairs_in(src, bank, a):
            block_ = src[:, bank, :].rearrange("p (a q i) -> p a q i", a=4, q=4)
            return block_[:, a % 4, :, 2 * a + 1:FEATURES]

        def pairs_out(a):
            return pairs[:, :, START[a]:START[a] + WIDTH[a]]

        def flat_a_in(src, parity):
            return src[:, 0, :].rearrange("p (q e g) -> p e q g", q=4, e=2)[:, parity]

        def flat_b_in(src, parity):
            return src[64:128, 1, :].rearrange("p (q e g) -> p e q g", q=4, e=2)[:, parity]

        def by_q(samples):
            return samples.rearrange("p (q g) -> p q g", q=4)

        x_in_vecs = vecs[:, :, :, 0].rearrange("p g q -> p q g")

        block = ctx.enter_context(nc.Block())

        @block.sync
        def _(sp):
            sp.dma_start(rows[:, :, :], indices).then_inc(idx_in, 16)
            for n, (kind, nrows, ncols) in enumerate(RAW):
                k = n - [r[0] for r in RAW].index(kind)
                if n >= SLOTS:
                    sp.wait_ge(low_made, n - SLOTS + 1)
                if kind in ("bot0", "dense"):
                    src = bot_w0 if kind == "bot0" else dense[:, k * STAGED:(k + 1) * STAGED]
                    for c in range(3):
                        sp.dma_start(staged[32 * c:32 * c + 32, n % SLOTS, 0:ncols], src)\
                          .then_inc(raw_in[n % SLOTS], 16)
                else:
                    src = {"bot1": bot_w1, "bot2": bot_w2}.get(kind)
                    if src is None:
                        src = (top_w0 if kind == "top0" else top_w1)[:, k, :]
                    sp.dma_start(staged[:, n % SLOTS, 0:ncols], src).then_inc(raw_in[n % SLOTS], 16)
                if n == 0:
                    sp.dma_start(cols[:, :], columns).then_inc(cols_in, 16)

            sp.wait_ge(act_done, PROLOGUE_USES + (TILES - 1) * LOOP_USES + len(EPILOGUE))
            sp.dma_start(out, probs[96:97, :]).then_inc(sent, 16)
            sp.wait_ge(sent, 16)

        @block.gpsimd
        def _(pool):
            nc.gpsimd.iota(base[:, 0:TILES * HALVES * TABLES], pattern=[[0, TILES * HALVES], [ROWS, TABLES]],
                           base=0, channel_multiplier=0)\
              .then_inc(const_made, 1)
            nc.gpsimd.memset(ones[:, :], 1.0).then_inc(const_made, 1)
            pool.wait_ge(const_made, 2)
            nc.gpsimd.affine_select(out=ident[:, :], in_=ones[:, :], compare_op=ALU.is_equal, fill=0.0,
                                    base=0, pattern=[[-1, P]], channel_multiplier=1)\
              .then_inc(const_made, 1)

            def gather_unit(h, u):
                first, count = UNITS[u]
                for f in range(first, first + count):
                    nc.gpsimd.indirect_dma_start(
                        out=ring[:, f, :], out_offset=None, in_=table_rows,
                        in_offset=bass.IndirectOffsetOnAxis(ap=row_now[h][:, f:f + 1], axis=0))\
                      .then_inc(gathered[u], 16)

            pool.wait_ge(row_ready[0], 1)
            pool.wait_ge(row_ready[1], 1)
            for u in range(len(UNITS)):
                gather_unit(0, u)
            for u in range(len(UNITS)):
                pool.wait_ge(turns, u + 1)
                gather_unit(1, u)
            units_turned = pool.alloc_register("units_turned")
            rows_given = pool.alloc_register("rows_given")
            pool.reg_mov(units_turned, len(UNITS))
            pool.reg_mov(rows_given, 1)
            with pool.Fori(1, TILES):
                pool.reg_add(rows_given, rows_given, 1)
                for h in range(HALVES):
                    for u in range(len(UNITS)):
                        pool.reg_add(units_turned, units_turned, 1)
                        pool.wait_ge(const_made, 3)
                        if u == 0:
                            pool.wait_ge(row_ready[h], rows_given)
                        pool.wait_ge(turns, units_turned)
                        gather_unit(h, u)

        @block.scalar
        def _(act):
            act.wait_ge(cols_in, 16)
            nc.scalar.activation(logit[:, 0:1], cols[0:1, 0:1], ACT.Sigmoid)
            for n in range(len(RAW)):
                slot, high, _ = raw_parts(n)
                act.wait_ge(raw_in[n % SLOTS], raw_count(n))
                nc.scalar.activation(high, slot, ACT.Copy).then_inc(high_made, 1)

            def turn(n, t):
                if n % 2 == 0:
                    act.wait_ge(turns, t * TILE_UNITS + n + 1)
                    nc.scalar.activation(vecs_out(n), turned_in(n), ACT.Copy).then_inc(act_kept, 1)

            def relu_of_bank0(high, src, col, m):
                nc.scalar.activation(relu[:, 0, :], src[:, 0, 0:TILE], ACT.Relu,
                                     bias=cols[:, col + m:col + m + 1])
                return nc.scalar.activation(high[:, m, :], src[:, 0, 0:TILE], ACT.Relu,
                                            bias=cols[:, col + m:col + m + 1])

            def use(kind, n, number, src, tile, first):
                act.wait_ge(filled, number + 1)
                if kind in SPLIT and not (first and number == 0):
                    act.wait_ge(dve_done, number)
                if kind == "bottom0":
                    last = relu_of_bank0(h0[:, 0], src, COL_B0, 2 * n)
                elif kind == "bottom1":
                    last = relu_of_bank0(h1[:, 0], src, COL_B1, 0)
                elif kind == "bottom2":
                    nc.scalar.activation(x_in_vecs, by_q(src[:, 0, 0:TILE]), ACT.Relu,
                                         bias=cols[:, COL_B2:COL_B2 + 1])
                    last = nc.scalar.activation(x[:, 0, :], src[:, 0, 0:TILE], ACT.Relu,
                                                bias=cols[:, COL_B2:COL_B2 + 1])
                elif kind == "dot":
                    for q in (0, 1):
                        last = nc.scalar.activation(dots_out(n, q), dots_in(src, q), ACT.Copy)
                elif kind == "pairs":
                    for a in ((0, 1, 2, 3), (8, 9, 10, 11))[n]:
                        last = nc.scalar.activation(pairs_out(a), pairs_in(src, 0, a), ACT.Copy)
                elif kind == "flat":
                    for e in range(2):
                        nc.scalar.activation(by_q(flat_a[:, 0, e, :]), flat_a_in(src, e), ACT.Copy)
                        last = nc.scalar.activation(by_q(flat_b[64 * e:64 * e + 64, 0, :]),
                                                    flat_b_in(src, e), ACT.Copy)
                elif kind == "top0":
                    last = relu_of_bank0(z0[:, 0], src, COL_T0, 2 * n)
                elif kind == "top1":
                    act.wait_ge(dve_done, number - 1)
                    for c in range(2):
                        m = 2 * n + c
                        last = nc.scalar.activation(z1[:, n % 2, c, :], src[:, c, 0:TILE], ACT.Relu,
                                                    bias=cols[:, COL_T1 + m:COL_T1 + m + 1])
                elif kind == "last":
                    act.wait_ge(dve_done, number + 1)
                    last = nc.scalar.activation(probs[96:97, bass.ds(tile * TILE, TILE)], logit[:, :],
                                                ACT.Sigmoid)
                last.then_inc(act_done, 1)

            def section(steps, start, start_pair, tile, turn_tile, first=False):
                at = 0
                for kind, n in steps:
                    if kind == "turn":
                        turn(n, turn_tile)
                    elif kind != "x part":
                        use(kind, n, start + at, banks[(start_pair + at) % 3], tile, first)
                        at += 1

            section(PROLOGUE, 0, 0, 0, 0, first=True)
            section(TO_TOP0, len(uses(PROLOGUE)), len(uses(PROLOGUE)), 0, 1)
            with act.Fori(0, TILES - 2) as t:
                start = PROLOGUE_USES + t * LOOP_USES
                section(LOOP, start, PROLOGUE_USES, t, t + 1)
                section(TO_TOP0, start + len(uses(LOOP)), PROLOGUE_USES + len(uses(LOOP)), t, t + 2)
            start = PROLOGUE_USES + (TILES - 2) * LOOP_USES
            section(LOOP, start, start, TILES - 2, TILES - 1)
            section(no_turns(TO_TOP0), start + len(uses(LOOP)), start + len(uses(LOOP)), TILES - 2, None)
            section(EPILOGUE, start + LOOP_USES, start, TILES - 1, None)

        @block.vector
        def _(dve):
            def make_rows(lo, hi, steps):
                part = rows[:, lo:hi, :].rearrange("p h t -> p (h t)")
                count = (hi - lo) * TABLES
                nc.vector.tensor_scalar(wrap[:, 0:count], part, 0.0, float(ROWS), ALU.is_lt, ALU.mult)\
                  .then_inc(rows_step, 1)
                dve.wait_ge(rows_step, steps + 1)
                nc.vector.tensor_tensor(part, part, wrap[:, 0:count], ALU.add).then_inc(rows_step, 1)
                dve.wait_ge(rows_step, steps + 2)
                nc.vector.tensor_scalar(part, part, 0.0, float(ROWS - 1), ALU.max, ALU.min)\
                  .then_inc(rows_step, 1)
                dve.wait_ge(rows_step, steps + 3)
                nc.vector.tensor_tensor(part, part, base[:, lo * TABLES:hi * TABLES], ALU.add)\
                  .then_inc(rows_step, 1)
                dve.wait_ge(rows_step, steps + 4)

            def give_rows(h, t):
                nc.vector.tensor_copy(row_now[h][:, :], rows[:, 2 * t + h, :].bitcast(U32))\
                  .then_inc(row_ready[h], 1)

            dve.wait_ge(idx_in, 16)
            dve.wait_ge(const_made, 1)
            make_rows(0, HALVES, 0)
            give_rows(0, 0)
            give_rows(1, 0)
            make_rows(HALVES, HALVES * TILES, 4)
            nc.vector.memset(vecs[:, :, :, FEATURES:PITCH], 0.0).then_inc(zero_made, 1)
            nc.vector.memset(pairs[:, :, HALF_PAIRS:PAIR_PITCH], 0.0).then_inc(zero_made, 1)
            for n, (kind, _, _) in enumerate(RAW):
                slot, high, low = raw_parts(n)
                dve.wait_ge(high_made, n + 1)
                if kind == "bot0":
                    low, high, slot = high[64:96], high[64:96], slot[64:96]
                elif kind == "dense":
                    low, high, slot = high[32:64], high[32:64], slot[32:64]
                nc.vector.tensor_tensor(low, slot, high.bitcast(F32), ALU.subtract).then_inc(low_made, 1)

            def turn(n, t):
                if n % 2:
                    dve.wait_ge(turns, t * TILE_UNITS + n + 1)
                    nc.vector.tensor_copy(vecs_out(n), turned_in(n)).then_inc(dve_kept, 1)

            def relu_of_bank1_and_low(both, src, col, m, number, splits):
                bias = cols[:, col + m + 1:col + m + 2]
                nc.vector.tensor_scalar(relu[:, 1, :], src[:, 1, 0:TILE], bias, 0.0, ALU.add, ALU.max)
                nc.vector.tensor_scalar(both[:, 0, m + 1, :], src[:, 1, 0:TILE], bias, 0.0,
                                        ALU.add, ALU.max).then_inc(relu_made, 1)
                dve.wait_ge(act_done, number + 1)
                dve.wait_ge(relu_made, splits + 1)
                return nc.vector.tensor_tensor(both[:, 1, m:m + 2, :], relu[:, :, :],
                                               both[:, 0, m:m + 2, :].bitcast(F32), ALU.subtract)

            def use(kind, n, number, src, splits, sums, first):
                dve.wait_ge(filled, number + 1)
                if kind in SPLIT and not (first and number == 0):
                    dve.wait_ge(dve_done, number)
                if kind == "bottom0":
                    last = relu_of_bank1_and_low(h0, src, COL_B0, 2 * n, number, splits)
                elif kind == "bottom1":
                    last = relu_of_bank1_and_low(h1, src, COL_B1, 0, number, splits)
                elif kind == "bottom2":
                    dve.wait_ge(act_done, number + 1)
                    last = nc.vector.tensor_tensor(by_q(x[:, 1, :]), x_in_vecs,
                                                   by_q(x[:, 0, :].bitcast(F32)), ALU.subtract)
                elif kind == "dot":
                    for q in (2, 3):
                        last = nc.vector.tensor_copy(dots_out(n, q), dots_in(src, q))
                elif kind == "pairs":
                    for a in ((4, 5, 6, 7), (12,))[n]:
                        last = nc.vector.tensor_copy(pairs_out(a), pairs_in(src, 1, a))
                elif kind == "flat":
                    dve.wait_ge(act_done, number + 1)
                    for e in range(2):
                        nc.vector.tensor_tensor(by_q(flat_a[:, 1, e, :]), flat_a_in(src, e),
                                                by_q(flat_a[:, 0, e, :].bitcast(F32)), ALU.subtract)
                        half = flat_b[64 * e:64 * e + 64]
                        last = nc.vector.tensor_tensor(by_q(half[:, 1, :]), flat_b_in(src, e),
                                                       by_q(half[:, 0, :].bitcast(F32)), ALU.subtract)
                elif kind == "top0":
                    last = relu_of_bank1_and_low(z0, src, COL_T0, 2 * n, number, splits)
                elif kind == "top1":
                    dve.wait_ge(act_done, number + 1)
                    w2 = cols[:, COL_W2 + 2 * n:COL_W2 + 2 * n + 2]
                    if n == 0:
                        nc.vector.tensor_scalar(weighted[:, :], z1[:, 0, 0, :], w2[:, 0:1], None, ALU.mult)\
                          .then_inc(weighted_made, 1)
                    else:
                        dve.wait_ge(dve_done, number)
                        nc.vector.scalar_tensor_tensor(weighted[:, :], z1[:, n % 2, 0, :], w2[:, 0:1],
                                                       weighted[:, :], ALU.mult, ALU.add)\
                          .then_inc(weighted_made, 1)
                    dve.wait_ge(weighted_made, sums + n + 1)
                    last = nc.vector.scalar_tensor_tensor(weighted[:, :], z1[:, n % 2, 1, :], w2[:, 1:2],
                                                          weighted[:, :], ALU.mult, ALU.add)
                elif kind == "last":
                    last = nc.vector.tensor_scalar(logit[:, :], src[0:1, 0, 0:TILE],
                                                   cols[0:1, COL_LAST:COL_LAST + 1], None, ALU.add)
                last.then_inc(dve_done, 1)

            def section(steps, start, start_pair, splits, tile, turn_tile, next_rows=True, first=False):
                at = 0
                for kind, n in steps:
                    if kind == "turn":
                        turn(n, turn_tile)
                        if n in (7, 13) and next_rows:
                            give_rows(0 if n == 7 else 1, turn_tile + 1)
                    elif kind != "x part":
                        use(kind, n, start + at, banks[(start_pair + at) % 3], splits, 4 * tile, first)
                        at += 1
                        splits = splits + (kind in SPLIT)

            section(PROLOGUE, 0, 0, 0, 0, 0, first=True)
            section(TO_TOP0, len(uses(PROLOGUE)), len(uses(PROLOGUE)), 3, 0, 1)
            with dve.Fori(0, TILES - 2) as t:
                start = PROLOGUE_USES + t * LOOP_USES
                section(LOOP, start, PROLOGUE_USES, 7 * t + 7, t, t + 1)
                section(TO_TOP0, start + len(uses(LOOP)), PROLOGUE_USES + len(uses(LOOP)), 7 * t + 10,
                        t, t + 2)
            t = TILES - 2
            start = PROLOGUE_USES + t * LOOP_USES
            section(LOOP, start, start, 7 * t + 7, t, t + 1, next_rows=False)
            section(no_turns(TO_TOP0), start + len(uses(LOOP)), start + len(uses(LOOP)), 7 * t + 10, t, None)
            section(EPILOGUE, start + LOOP_USES, start, 7 * t + 14, TILES - 1, None)

        @block.tensor
        def _(pe):
            def split_product(dst, weights, values, first=True, last=True):
                terms = [(w, v) for (wh, wl), (vh, vl) in zip(weights, values)
                         for w, v in ((wh, vh), (wh, vl), (wl, vh))]
                for k, (w, v) in enumerate(terms):
                    ins = nc.tensor.matmul(dst, w, v, start=first and k == 0,
                                           stop=last and k == len(terms) - 1)
                return ins

            def turn(n, t, first):
                h, u = n // len(UNITS), n % len(UNITS)
                if not (first and n < 2):
                    pe.wait_ge(dve_kept if n % 2 else act_kept, t * (TILE_UNITS // 2) + n // 2)
                pe.wait_ge(gathered[u], 16 * UNITS[u][1] * (HALVES * t + h + 1))
                for c in range(UNITS[u][1]):
                    last = nc.tensor.transpose(turned[n % 2][:, c, :], ring[:, UNITS[u][0] + c, :],
                                               ident[:, :])
                last.then_inc(turns, 1)

            def chunk(w, k, m):
                return w[:, 0, k, m * P:m * P + P], w[:, 1, k, m * P:m * P + P]

            def x_part(n, dst):
                for c in range(2):
                    split_product(dst[:, c, 0:TILE], [chunk(w_top0, 0, 2 * n + c)],
                                  [(x[:, 0, :], x[:, 1, :])], last=False)

            def use(kind, n, dst, tile):
                if kind == "bottom0":
                    for c in range(2):
                        m = 2 * n + c
                        last = nc.tensor.matmul(dst[:, c, 0:TILE], w_bot0[:, m * P:m * P + P],
                                                dense_hlh[:, bass.ds(tile * TILE, TILE)],
                                                start=True, stop=True)
                elif kind == "bottom1":
                    for m in range(2):
                        last = split_product(dst[:, m, 0:TILE], [chunk(w_bot1, k, m) for k in range(M1)],
                                             [(h0[:, 0, k, :], h0[:, 1, k, :]) for k in range(M1)])
                elif kind == "bottom2":
                    last = split_product(dst[:, 0, 0:TILE], [chunk(w_bot2, k, 0) for k in range(M2)],
                                         [(h1[:, 0, k, :], h1[:, 1, k, :]) for k in range(M2)])
                elif kind == "dot":
                    for g in range(8):
                        group = vecs[:, 8 * n + g, :, :]
                        last = nc.tensor.matmul(
                            dst[:, g // 4, g % 4 * P:g % 4 * P + 4 * FEATURES],
                            group.rearrange("p q f -> p (q f)"), group[:, :, 0:FEATURES],
                            start=True, stop=True)
                elif kind == "pairs":
                    for k, a in enumerate((range(8), range(8, 13))[n]):
                        last = nc.tensor.transpose(
                            dst[:, k // 4, k % 4 * P:k % 4 * P + P],
                            dots[:, 2 * a:2 * a + 2, :].rearrange("p e g -> p (e g)"), ident[:, :])
                elif kind == "flat":
                    for b, at in enumerate((0, PAIR_PITCH - P)):
                        for q in range(4):
                            last = nc.tensor.transpose(dst[:, b, q * P:q * P + P],
                                                       pairs[:, q, at:at + P], ident[:, :])
                elif kind == "top0":
                    if n >= 2:
                        x_part(n, dst)
                    for c in range(2):
                        m = 2 * n + c
                        last = split_product(
                            dst[:, c, 0:TILE], [chunk(w_top0, k, m) for k in (1, 2, 3)],
                            [(flat_a[:, 0, e, :], flat_a[:, 1, e, :]) for e in range(2)]
                            + [(flat_b[:, 0, :], flat_b[:, 1, :])], first=False)
                elif kind == "top1":
                    for c in range(2):
                        m = 2 * n + c
                        last = split_product(dst[:, c, 0:TILE], [chunk(w_top1, k, m) for k in range(MT)],
                                             [(z0[:, 0, k, :], z0[:, 1, k, :]) for k in range(MT)])
                elif kind == "last":
                    last = nc.tensor.matmul(dst[:, 0, 0:TILE], ones[:, :], weighted[:, :],
                                            start=True, stop=True)
                last.then_inc(filled, 1)

            def done(number):
                pe.wait_ge(act_done, number + 1)
                pe.wait_ge(dve_done, number + 1)

            def section(steps, start, start_pair, turn_tile, dense_tile, first=False):
                made = {}
                order = uses(steps)
                at = 0
                for kind, n in steps:
                    if kind == "turn":
                        turn(n, turn_tile, first)
                        continue
                    k = order.index(("top0", n)) if kind == "x part" else at
                    needed = max(k - 3, made.get(NEEDS.get(kind), k - 3),
                                 -1 if (kind, n) in (("top1", 0), ("pairs", 0)) else k - 3)
                    if needed >= 0 or not first:
                        done(start + needed)
                    if kind == "dot" and n == 0:
                        pe.wait_ge(act_kept, (turn_tile + 1) * (TILE_UNITS // 2))
                        pe.wait_ge(dve_kept, (turn_tile + 1) * (TILE_UNITS // 2))
                    if kind == "x part":
                        x_part(n, banks[(start_pair + k) % 3])
                        continue
                    use(kind, n, banks[(start_pair + k) % 3], dense_tile)
                    made[kind] = k
                    at += 1

            pe.wait_ge(const_made, 3)
            pe.wait_ge(zero_made, 2)
            pe.wait_ge(low_made, len(RAW))
            section(PROLOGUE, 0, 0, 0, 0, first=True)
            section(TO_TOP0, len(uses(PROLOGUE)), len(uses(PROLOGUE)), 1, None)
            with pe.Fori(0, TILES - 2) as t:
                start = PROLOGUE_USES + t * LOOP_USES
                section(LOOP, start, PROLOGUE_USES, t + 1, t + 1)
                section(TO_TOP0, start + len(uses(LOOP)), PROLOGUE_USES + len(uses(LOOP)), t + 2, None)
            t = TILES - 2
            start = PROLOGUE_USES + t * LOOP_USES
            section(LOOP, start, start, t + 1, t + 1)
            section(no_turns(TO_TOP0), start + len(uses(LOOP)), start + len(uses(LOOP)), None, None)
            section(EPILOGUE, start + LOOP_USES, start, None, None)


def lay_out(inputs):
    import numpy as np

    def chunks(w):
        return np.ascontiguousarray(w.T.reshape(-1, P, w.shape[0]).transpose(1, 0, 2))

    def padded(w, n=PITCH):
        wide = np.zeros((n, w.shape[0]), w.dtype)
        wide[0:w.shape[1]] = w.T
        return wide

    a = {k.removeprefix("L0_rec_"): np.asarray(v) for k, v in inputs.items()}
    w0 = a["top_w0"]
    top_w0 = np.zeros((P, 4, TOP), w0.dtype)
    top_w0[:, 0] = w0[:, 0:D].T
    for j in range(TABLES):
        for i in range(j + 1, FEATURES):
            r = START[j // 2] + i - (j // 2 * 2 + 1)
            column = w0[:, D + i * (i - 1) // 2 + j]
            if r < P:
                top_w0[r, 1 + j % 2] = column
            else:
                top_w0[r - P + 64 * (j % 2), 3] = column
    columns = np.zeros((P, COLUMNS), np.float32)
    for at, v in ((COL_B0, a["bot_b0"]), (COL_B1, a["bot_b1"]), (COL_B2, a["bot_b2"]),
                  (COL_T0, a["top_b0"]), (COL_T1, a["top_b1"]), (COL_W2, a["top_w2"][0])):
        columns[:, at:at + v.size // P] = v.reshape(-1, P).T
    columns[0, COL_LAST] = a["top_b2"][0]
    return {
        "indices": np.ascontiguousarray(a["r_lS_i"].reshape(TABLES, -1, P).transpose(2, 1, 0)),
        "tables": np.ascontiguousarray(a["emb_W"]),
        "dense": padded(a["r_dense_x"]),
        "bot_w0": padded(a["bot_w0"]),
        "bot_w1": chunks(a["bot_w1"]),
        "bot_w2": chunks(a["bot_w2"]),
        "top_w0": top_w0,
        "top_w1": chunks(a["top_w1"]),
        "columns": columns,
    }


def kernel(**inputs):
    import concourse.bacc as bacc
    from concourse.bass_utils import run_bass_kernel_spmd

    nc = bacc.Bacc("TRN2", target_bir_lowering=False, num_devices=1)
    arrays = lay_out(inputs)
    args = [nc.dram_tensor(n, v.shape, mybir.dt.from_np(v.dtype), kind="ExternalInput").ap()
            for n, v in arrays.items()]
    out = nc.dram_tensor("out", (1, BATCH), F32, kind="ExternalOutput").ap()
    dlrm(nc, *args, out)
    r = run_bass_kernel_spmd(nc, [arrays], core_ids=[0])
    return r.results[0]["out"].reshape(BATCH, 1)
```

```python
import concourse.bass as bass
from concourse import mybir
from contextlib import ExitStack

F32, F32R = mybir.dt.float32, mybir.dt.float32r
I32, U32 = mybir.dt.int32, mybir.dt.uint32
ACT, ALU = mybir.ActivationFunctionType, mybir.AluOpType

P = 128
BATCH, TABLES, ROWS, D = 2048, 26, 12500, 128
DENSE, BOT1, BOT2 = 13, 512, 256
TOP = 1024
TILE = 256
TILES = BATCH // TILE
HALVES = TILE // P
GROUPS = TILE // 4
PITCH = 32
FEATURES = TABLES + 1
DOT_ROWS = 3 * PITCH + FEATURES
M1, M2, MT = BOT1 // P, BOT2 // P, TOP // P
ROUND = 512
ROUNDS = BATCH // ROUND
WIDTH = [FEATURES - 1 - 2 * a for a in range(TABLES // 2)]
START = [sum(WIDTH[:a]) for a in range(TABLES // 2)]
HALF_PAIRS = sum(WIDTH)
PAIR_PITCH = 192
UNITS = [(4 * u, min(4, TABLES - 4 * u)) for u in range(7)]
NU = len(UNITS)
TILE_UNITS = HALVES * NU
COL_B1, COL_B2, COL_LAST = 0, M2, M2 + 1
COLUMNS = COL_LAST + 1
STAGED = 1024
SLOTS = 4

OTHERS = ("turn", "split", "zeros", "x in vecs", "x", "quarter", "half")


def bottom(r):
    layer0 = [("bottom0", 2 * r + 2, (r + 1) % 3), ("bottom0", 2 * r + 3, (r + 2) % 3)]
    if r == ROUNDS - 1:
        return [("bottom1", r, r % 3), ("turn", 2 * r), ("turn", 2 * r + 1), ("bottom2", r, r % 3)]
    return [layer0[0], ("bottom1", r, r % 3), layer0[1], ("turn", 2 * r), ("split", 5 + r), ("half", r + 1),
            ("turn", 2 * r + 1), ("bottom2", r, r % 3)]


PROLOGUE = ([("split", 0), ("split", 1), ("split", 2), ("bottom0", 0, 2), ("bottom0", 1, 1), ("half", 0),
             ("split", 3), ("zeros",), ("split", 4)] + sum((bottom(r) for r in range(ROUNDS)), [])
            + [("x in vecs",), ("split", 8), ("dot", 0, 1), ("split", 9), ("dot", 1, 2), ("split", 10), ("dot", 2, 1),
               ("turn", 8), ("dot", 3, 2), ("split", 11), ("turn", 9), ("turn", 10), ("x",),
               ("turn", 11), ("turn", 12), ("turn", 13)])
BODY = [
    ("dot", 4, 0), ("dot", 5, 1), ("turn", 0), ("dot", 6, 0), ("dot", 7, 1),
    ("quarter", 1, 2), ("pairs", 0, 0), ("pairs", 1, 1), ("turn", 1), ("turn", 2),
    ("flat", 0, 0), ("x in vecs",), ("top1", 1, 2), ("turn", 3),
    ("top0", 0, 1), ("turn", 4), ("top0", 1, 0), ("turn", 5), ("top0", 2, 2), ("turn", 6), ("top0", 3, 1),
    ("dot", 0, 0), ("dot", 1, 2), ("turn", 7), ("dot", 2, 0), ("dot", 3, 2), ("x",), ("turn", 8),
    ("quarter", 0, 0), ("quarter", 0, 1), ("turn", 9), ("quarter", 0, 2), ("turn", 10), ("top1", 0, 1),
    ("quarter", 1, 0), ("turn", 11), ("turn", 12), ("turn", 13), ("quarter", 1, 1)]
FIRST = [("split", 12)] + sum(([s, ("split", 9 + s[1])] if s[:1] == ("dot",) and s[1] >= 4 else [s]
                               for s in BODY if s not in (("quarter", 1, 2), ("top1", 1, 2))), [])
LAST = [s for s in BODY[:BODY.index(("dot", 0, 0))] if s[0] not in ("turn", "x in vecs")] + [
    ("quarter", 0, 0), ("quarter", 0, 1), ("quarter", 0, 2), ("top1", 0, 0),
    ("quarter", 1, 0), ("quarter", 1, 1), ("quarter", 1, 2), ("top1", 1, 2)]
LOOPED = TILES - 2


def uses(steps):
    return [s for s in steps if s[0] not in OTHERS]


def uses_named(steps):
    return [s[:2] for s in uses(steps)]


def by_act(steps):
    return sum(s[0] != "top1" for s in uses(steps))


def by_dve(steps):
    return sum(s[0] != "bottom2" for s in uses(steps))


def top1_steps(steps):
    return 2 * sum(s[0] == "top1" for s in steps)


def totals(steps_before):
    steps = sum(steps_before, [])
    return (len(uses(steps)), by_act(steps), by_dve(steps),
            top1_steps(steps) + sum(s[0] == "bottom1" for s in steps))


AT_FIRST = totals([PROLOGUE])
AT_LOOP = totals([PROLOGUE, FIRST])
IN_LOOP = totals([BODY])
AT_LAST = tuple(a + LOOPED * b for a, b in zip(AT_LOOP, IN_LOOP))
AT_END = tuple(a + b for a, b in zip(AT_LAST, totals([LAST])))

NEEDS = {"bottom2": "bottom1", "flat": "pairs", "top0": "flat", "pairs": "dot"}


def dlrm(nc, indices, tables, dense, bot_w0, bot_w1, bot_w2, top_w0, top_w1, columns, top_b1, top_w2, out):
    table_rows = tables.rearrange("t r d -> (t r) d")
    ctx = ExitStack()
    with ctx:
        def sb(name, shape, dt):
            return ctx.enter_context(nc.sbuf_tensor(name, shape, dt))

        def sem(name):
            return ctx.enter_context(nc.semaphore(name))

        z0_at = (nc.sbuf_base + 31) // 32 * 32
        sb("z0_region", [P, 2 * MT * TILE], F32)
        staged = nc.alloc_sbuf_tensor_at("staged", [P, SLOTS, STAGED], F32, offset=z0_at)
        z0 = nc.alloc_sbuf_tensor_at("z0", [P, 2, MT, TILE], F32R, offset=z0_at)
        w_top1_at = (nc.sbuf_base + 31) // 32 * 32
        sb("w_top1_region", [P, 2 * MT * TOP], F32)
        w_top1 = nc.alloc_sbuf_tensor_at("w_top1", [P, 2, MT, TOP], F32R, offset=w_top1_at)
        next_at = [w_top1_at]

        def early(name, shape, dt=F32R):
            at = next_at[0]
            words = 1
            for n in shape[1:]:
                words *= n
            next_at[0] += 4 * words
            return nc.alloc_sbuf_tensor_at(name, shape, dt, offset=at)

        w_bot0 = early("w_bot0", [96, BOT1])
        dense_hlh = early("dense_hlh", [96, BATCH])
        w_bot1 = early("w_bot1", [P, 2, M1, BOT2])
        w_bot2 = early("w_bot2", [P, 2, M2, D])
        h0 = early("h0", [P, 2, 2, M1, ROUND])
        h1 = early("h1", [P, 2, M2, ROUND])
        relu = early("relu", [P, 2, ROUND], F32)
        assert next_at[0] <= w_top1_at + 8 * MT * TOP

        ring = sb("ring", [P, TABLES, D], F32)
        vecs = sb("vecs", [P, GROUPS, 4, PITCH], F32)
        dots = sb("dots", [P, TABLES, GROUPS], F32)
        w_top0 = sb("w_top0", [P, 2, 4, TOP], F32R)
        x_all = sb("x_all", [P, BATCH], F32)
        x = sb("x", [P, 2, TILE], F32R)
        flat_a = sb("flat_a", [P, 2, 2, TILE], F32R)
        flat_b = sb("flat_b", [P, 2, TILE], F32R)
        pairs = sb("pairs", [P, 4, PAIR_PITCH], F32)
        hidden = sb("hidden", [P, 2, TOP // 2], F32)
        weighed = sb("weighed", [P, 2, TOP // 2], F32)
        sums = sb("sums", [P, 2], F32)
        b1_rows = sb("b1_rows", [P, 2, TOP // 2], F32)
        w2_rows = sb("w2_rows", [P, 2, TOP // 2], F32)
        logits = sb("logits", [P, BATCH // P], F32)
        probs = sb("probs", [P, BATCH // P], F32)
        rows = sb("rows", [P, (TILES + 1) * HALVES, TABLES], I32)
        row_now = [sb(f"row_now{h}", [P, TABLES], U32) for h in range(HALVES)]
        cols = sb("cols", [P, COLUMNS], F32)
        ident = sb("ident", [P, P], F32)
        wrap = hidden[:, :, :].bitcast(I32).rearrange("p a n -> p (a n)")
        base = weighed[:, :, :].bitcast(I32).rearrange("p a n -> p (a n)")

        turned = [ctx.enter_context(nc.psum_tensor(f"turned{n}", [P, 4, P], F32)) for n in range(2)]
        banks = [ctx.enter_context(nc.psum_tensor(f"banks{n}", [P, 2, 512], F32)) for n in range(3)]

        idx_in, cols_in, rows_in = sem("idx_in"), sem("cols_in"), sem("rows_in")
        raw_in = [sem(f"raw_in{n}") for n in range(SLOTS)]
        high_made, low_made = sem("high_made"), sem("low_made")
        const_made = sem("const_made")
        zero_made = sem("zero_made")
        rows_step = sem("rows_step")
        row_ready = [sem(f"row_ready{h}") for h in range(HALVES)]
        gathered = [sem(f"gathered{u}") for u in range(NU)]
        turns = sem("turns")
        act_kept, dve_kept = sem("act_kept"), sem("dve_kept")
        x_kept = sem("x_kept")
        x_high, x_low = sem("x_high"), sem("x_low")
        filled = sem("filled")
        act_done, dve_done = sem("act_done"), sem("dve_done")
        dve_step = sem("dve_step")
        probs_made, sent = sem("probs_made"), sem("sent")

        RAW = ([("bot0", 0, 96, BOT1), ("dense", 0, 96, STAGED), ("bot1", 0, P, M1 * BOT2),
                ("bot2", 0, P, M2 * D), ("dense", 1, 96, STAGED)]
               + [("top0", k, P, TOP) for k in range(4)] + [("top1", k, P, TOP) for k in range(MT)])
        RAW_DMAS = [3 if nrows == 96 else 1 for _, _, nrows, _ in RAW]

        def raw_parts(n):
            kind, k, nrows, ncols = RAW[n]
            slot = staged[0:nrows, n % SLOTS, 0:ncols]
            if kind == "bot0":
                return slot, w_bot0[:, :], None
            if kind == "dense":
                return slot, dense_hlh[:, k * STAGED:(k + 1) * STAGED], None
            if kind in ("bot1", "bot2"):
                w = w_bot1 if kind == "bot1" else w_bot2
                return slot, *(w[:, s, :, :].rearrange("p k m -> p (k m)") for s in range(2))
            w = w_top0 if kind == "top0" else w_top1
            return slot, w[:, 0, k, :], w[:, 1, k, :]

        def raw_count(n):
            return 16 * sum(RAW_DMAS[n % SLOTS:n + 1:SLOTS])

        def vecs_out(n):
            h, (first, count) = n // NU, UNITS[n % NU]
            return vecs[:, 32 * h:32 * h + 32, :, 1 + first:1 + first + count].rearrange("p g q f -> p f q g")

        def turned_in(n):
            return turned[n % 2][:, 0:UNITS[n % NU][1], :].rearrange("p f (q g) -> p f q g", q=4)

        def dots_in(src, q):
            groups = src[32 * q:32 * q + (32 if q < 3 else FEATURES), :, :].rearrange("i b (g c) -> i (b g) c", g=4)
            return groups[:, :, q * TABLES:(q + 1) * TABLES]

        def dots_out(n, q):
            return dots[32 * q:32 * q + (32 if q < 3 else FEATURES), :, 8 * n:8 * n + 8].rearrange("i j g -> i g j")

        def pairs_in(src, bank, a):
            block_ = src[:, bank, :].rearrange("p (a q i) -> p a q i", a=4, q=4)
            return block_[:, a % 4, :, 2 * a + 1:FEATURES]

        def pairs_out(a):
            return pairs[:, :, START[a]:START[a] + WIDTH[a]]

        def flat_a_in(src, parity):
            return src[:, 0, :].rearrange("p (q e g) -> p e q g", q=4, e=2)[:, parity]

        def flat_b_in(src, parity):
            return src[64:128, 1, :].rearrange("p (q e g) -> p e q g", q=4, e=2)[:, parity]

        def by_q(samples):
            return samples.rearrange("p (q g) -> p q g", q=4)

        x_in_vecs = vecs[:, :, :, 0].rearrange("p g q -> p q g")

        def x_of(tile):
            return x_all[:, bass.ds(tile * TILE, TILE)]

        def z0_use(n, part):
            return z0[:, part, 2 * n:2 * n + 2, :]

        block = ctx.enter_context(nc.Block())

        @block.sync
        def _(sp):
            sp.dma_start(rows[:, 0:TILES * HALVES, :], indices).then_inc(idx_in, 16)
            for n, (kind, k, nrows, ncols) in enumerate(RAW):
                if n >= SLOTS:
                    sp.wait_ge(low_made, n - SLOTS + 1)
                if kind in ("bot0", "dense"):
                    src = bot_w0 if kind == "bot0" else dense[:, k * STAGED:(k + 1) * STAGED]
                    for c in range(3):
                        sp.dma_start(staged[32 * c:32 * c + 32, n % SLOTS, 0:ncols], src)\
                          .then_inc(raw_in[n % SLOTS], 16)
                else:
                    src = {"bot1": bot_w1, "bot2": bot_w2}.get(kind)
                    if src is None:
                        src = (top_w0 if kind == "top0" else top_w1)[:, k, :]
                    sp.dma_start(staged[:, n % SLOTS, 0:ncols], src).then_inc(raw_in[n % SLOTS], 16)
                if n == 0:
                    sp.dma_start(cols[:, :], columns).then_inc(cols_in, 16)
                if n == 8:
                    for row, values in ((b1_rows, top_b1), (w2_rows, top_w2)):
                        sp.dma_start(row[:, :, :].rearrange("p a n -> p (a n)"),
                                     values.to_broadcast([P, TOP])).then_inc(rows_in, 16)
            sp.wait_ge(probs_made, 1)
            sp.dma_start(out, probs[:, :]).then_inc(sent, 16)
            sp.wait_ge(sent, 16)

        @block.gpsimd
        def _(pool):
            nc.gpsimd.iota(base[:, 0:TILES * HALVES * TABLES], pattern=[[0, TILES * HALVES], [ROWS, TABLES]],
                           base=0, channel_multiplier=0).then_inc(const_made, 1)
            nc.gpsimd.memset(ident[:, :], 0.0).then_inc(const_made, 1)
            pool.wait_ge(const_made, 2)
            nc.gpsimd.affine_select(out=ident[:, :], in_=ident[:, :], compare_op=ALU.not_equal, fill=1.0,
                                    base=0, pattern=[[-1, P]], channel_multiplier=1)\
              .then_inc(const_made, 1)

            def gather_unit(h, u):
                first, count = UNITS[u]
                for f in range(first, first + count):
                    nc.gpsimd.indirect_dma_start(
                        out=ring[:, f, :], out_offset=None, in_=table_rows,
                        in_offset=bass.IndirectOffsetOnAxis(ap=row_now[h][:, f:f + 1], axis=0))\
                      .then_inc(gathered[u], 16)

            pool.wait_ge(row_ready[0], 1)
            pool.wait_ge(row_ready[1], 1)
            for u in range(NU):
                gather_unit(0, u)
            for u in range(NU):
                pool.wait_ge(turns, u + 1)
                gather_unit(1, u)
            units_turned = pool.alloc_register("units_turned")
            rows_given = pool.alloc_register("rows_given")
            pool.reg_mov(units_turned, NU)
            pool.reg_mov(rows_given, 1)
            with pool.Fori(1, TILES):
                pool.reg_add(rows_given, rows_given, 1)
                for h in range(HALVES):
                    for u in range(NU):
                        pool.reg_add(units_turned, units_turned, 1)
                        pool.wait_ge(const_made, 3)
                        if u == 0:
                            pool.wait_ge(row_ready[h], rows_given)
                        pool.wait_ge(turns, units_turned)
                        gather_unit(h, u)

        @block.scalar
        def _(act):
            act.wait_ge(cols_in, 16)
            nc.scalar.activation(probs[:, 0:1], cols[:, 0:1], ACT.Sigmoid)

            def split(n):
                slot, high, _ = raw_parts(n)
                act.wait_ge(raw_in[n % SLOTS], raw_count(n))
                nc.scalar.activation(high, slot, ACT.Copy).then_inc(high_made, 1)

            def turn(n, t):
                if n % 2 == 0:
                    act.wait_ge(turns, t * TILE_UNITS + n + 1)
                    nc.scalar.activation(vecs_out(n), turned_in(n), ACT.Copy).then_inc(act_kept, 1)

            def keep_x(tile):
                nc.scalar.activation(x_in_vecs, by_q(x_of(tile)), ACT.Copy).then_inc(x_kept, 1)

            def take_x(tile):
                nc.scalar.activation(x[:, 0, :], x_of(tile), ACT.Copy).then_inc(x_high, 1)

            def use(kind, n, number, src, first):
                act.wait_ge(filled, number + 1)
                if kind == "bottom0":
                    m = n % 2 * 2
                    last = nc.scalar.activation(h0[:, n // 2 % 2, 0, m:m + 2, :], src[:, :, :], ACT.Relu)
                elif kind == "bottom1":
                    bias = cols[:, COL_B1:COL_B1 + 1]
                    nc.scalar.activation(relu[:, 0, :], src[:, 0, :], ACT.Relu, bias=bias)
                    last = nc.scalar.activation(h1[:, 0, 0, :], src[:, 0, :], ACT.Relu, bias=bias)
                elif kind == "bottom2":
                    last = nc.scalar.activation(x_all[:, n * ROUND:(n + 1) * ROUND], src[:, 0, :], ACT.Relu,
                                                bias=cols[:, COL_B2:COL_B2 + 1])
                elif kind == "dot":
                    for q in (0, 1):
                        last = nc.scalar.activation(dots_out(n, q), dots_in(src, q), ACT.Copy)
                elif kind == "pairs":
                    for a in ((0, 1, 2, 3), (8, 9, 10, 11))[n]:
                        last = nc.scalar.activation(pairs_out(a), pairs_in(src, 0, a), ACT.Copy)
                elif kind == "flat":
                    for e in range(2):
                        nc.scalar.activation(by_q(flat_a[:, 0, e, :]), flat_a_in(src, e), ACT.Copy)
                        last = nc.scalar.activation(by_q(flat_b[64 * e:64 * e + 64, 0, :]),
                                                    flat_b_in(src, e), ACT.Copy)
                elif kind == "top0":
                    if first:
                        act.wait_ge(low_made, len(RAW))
                    last = nc.scalar.activation(z0_use(n, 0), src[:, :, 0:TILE], ACT.Relu)
                last.then_inc(act_done, 1)

            def section(steps, before, turn_tile):
                number = before[0]
                for kind, *n in steps:
                    if kind == "turn":
                        turn(n[0], turn_tile)
                    elif kind == "split":
                        split(n[0])
                    elif kind == "x in vecs":
                        keep_x(turn_tile)
                    elif kind == "x":
                        take_x(turn_tile)
                    elif kind not in OTHERS:
                        if kind != "top1":
                            use(kind, n[0], number, banks[n[1]], steps is FIRST)
                        number = number + 1

            section(PROLOGUE, (0, 0, 0, 0), 0)
            section(FIRST, AT_FIRST, 1)
            with act.Fori(0, LOOPED) as t:
                section(BODY, [a + t * b for a, b in zip(AT_LOOP, IN_LOOP)], t + 2)
            section(LAST, AT_LAST, None)
            act.wait_ge(dve_done, AT_END[2])
            nc.scalar.activation(probs[:, :], logits[:, :], ACT.Sigmoid, bias=cols[:, COL_LAST:COL_LAST + 1])\
              .then_inc(probs_made, 1)

        @block.vector
        def _(dve):
            def make_rows(lo, hi, steps):
                part = rows[:, lo:hi, :].rearrange("p h t -> p (h t)")
                count = (hi - lo) * TABLES
                nc.vector.tensor_scalar(wrap[:, 0:count], part, 0.0, float(ROWS), ALU.is_lt, ALU.mult)\
                  .then_inc(rows_step, 1)
                dve.wait_ge(rows_step, steps + 1)
                nc.vector.tensor_tensor(part, part, wrap[:, 0:count], ALU.add).then_inc(rows_step, 1)
                dve.wait_ge(rows_step, steps + 2)
                nc.vector.tensor_scalar(part, part, 0.0, float(ROWS - 1), ALU.max, ALU.min)\
                  .then_inc(rows_step, 1)
                dve.wait_ge(rows_step, steps + 3)
                nc.vector.tensor_tensor(part, part, base[:, lo * TABLES:hi * TABLES], ALU.add)\
                  .then_inc(rows_step, 1)
                dve.wait_ge(rows_step, steps + 4)

            def give_rows(h, t):
                nc.vector.tensor_copy(row_now[h][:, :], rows[:, 2 * t + h, :].bitcast(U32))\
                  .then_inc(row_ready[h], 1)

            dve.wait_ge(idx_in, 16)
            dve.wait_ge(const_made, 1)
            make_rows(0, HALVES, 0)
            give_rows(0, 0)
            give_rows(1, 0)

            def zeros():
                nc.vector.memset(vecs[:, :, :, FEATURES:PITCH], 0.0)
                nc.vector.memset(dots[96:128, :, :], 0.0)
                nc.vector.memset(pairs[:, :, HALF_PAIRS:HALF_PAIRS + 1], 1.0)
                nc.vector.memset(pairs[:, :, HALF_PAIRS + 1:PAIR_PITCH], 0.0).then_inc(zero_made, 1)
                make_rows(HALVES, HALVES * TILES, 4)
                nc.vector.memset(rows[:, HALVES * TILES:, :], 0)

            def split(n):
                slot, high, low = raw_parts(n)
                dve.wait_ge(high_made, n + 1)
                if RAW[n][0] == "bot0":
                    low, high, slot = high[64:96], high[64:96], slot[64:96]
                elif RAW[n][0] == "dense":
                    low, high, slot = high[32:64], high[32:64], slot[32:64]
                nc.vector.tensor_tensor(low, slot, high.bitcast(F32), ALU.subtract).then_inc(low_made, 1)

            def turn(n, t):
                if n % 2:
                    dve.wait_ge(turns, t * TILE_UNITS + n + 1)
                    nc.vector.tensor_copy(vecs_out(n), turned_in(n)).then_inc(dve_kept, 1)

            def take_x(tile):
                dve.wait_ge(x_high, tile + 1)
                nc.vector.tensor_tensor(x[:, 1, :], x_of(tile), x[:, 0, :].bitcast(F32), ALU.subtract)\
                  .then_inc(x_low, 1)

            def relu_low(low, src, high):
                return nc.vector.scalar_tensor_tensor(low, src, 0.0, high.bitcast(F32), ALU.max, ALU.subtract)

            def use(kind, n, number, src, acts, steps, column):
                dve.wait_ge(filled, number + 1)
                if kind in ("bottom0", "flat", "top0"):
                    dve.wait_ge(act_done, acts)
                if kind == "bottom0":
                    m = n % 2 * 2
                    out0 = h0[:, n // 2 % 2, :, m:m + 2, :]
                    last = relu_low(out0[:, 1], src[:, :, :], out0[:, 0])
                elif kind == "bottom1":
                    bias = cols[:, COL_B1 + 1:COL_B1 + 2]
                    nc.vector.tensor_scalar(relu[:, 1, :], src[:, 1, :], bias, 0.0, ALU.add, ALU.max)
                    nc.vector.tensor_scalar(h1[:, 0, 1, :], src[:, 1, :], bias, 0.0, ALU.add, ALU.max)\
                      .then_inc(dve_step, 1)
                    dve.wait_ge(act_done, acts)
                    dve.wait_ge(dve_step, steps + 1)
                    last = nc.vector.tensor_tensor(h1[:, 1, :, :], relu[:, :, :],
                                                   h1[:, 0, :, :].bitcast(F32), ALU.subtract)
                elif kind == "dot":
                    for q in (2, 3):
                        last = nc.vector.tensor_copy(dots_out(n, q), dots_in(src, q))
                elif kind == "pairs":
                    for a in ((4, 5, 6, 7), (12,))[n]:
                        last = nc.vector.tensor_copy(pairs_out(a), pairs_in(src, 1, a))
                elif kind == "flat":
                    for e in range(2):
                        nc.vector.tensor_tensor(by_q(flat_a[:, 1, e, :]), flat_a_in(src, e),
                                                by_q(flat_a[:, 0, e, :].bitcast(F32)), ALU.subtract)
                        half = flat_b[64 * e:64 * e + 64]
                        last = nc.vector.tensor_tensor(by_q(half[:, 1, :]), flat_b_in(src, e),
                                                       by_q(half[:, 0, :].bitcast(F32)), ALU.subtract)
                elif kind == "top0":
                    last = relu_low(z0_use(n, 1), src[:, :, 0:TILE], z0_use(n, 0))
                elif kind == "top1":
                    nc.vector.tensor_tensor(hidden[:, :, :], src[:, :, :], b1_rows[:, :, :], ALU.add)\
                      .then_inc(dve_step, 1)
                    dve.wait_ge(dve_step, steps + 1)
                    for half in range(2):
                        last = nc.vector.scalar_tensor_tensor(
                            weighed[:, half, :], hidden[:, half, :], 0.0, w2_rows[:, half, :],
                            ALU.max, ALU.mult, accum_out=sums[:, half:half + 1])
                    last.then_inc(dve_step, 1)
                    dve.wait_ge(dve_step, steps + 2)
                    last = nc.vector.tensor_tensor(logits[:, bass.ds(column, 1)], sums[:, 0:1],
                                                   sums[:, 1:2], ALU.add)
                last.then_inc(dve_done, 1)

            def section(steps, before, turn_tile, column):
                number, acts, _, own = before
                for kind, *n in steps:
                    if kind == "turn":
                        turn(n[0], turn_tile)
                        if n[0] in (7, 13):
                            give_rows(0 if n[0] == 7 else 1, turn_tile + 1)
                    elif kind == "split":
                        split(n[0])
                    elif kind == "zeros":
                        zeros()
                    elif kind == "x":
                        take_x(turn_tile)
                    elif kind not in OTHERS:
                        acts = acts + (kind != "top1")
                        if kind != "bottom2":
                            use(kind, n[0], number, banks[n[1]], acts, own, column)
                        own = own + {"bottom1": 1, "top1": 2}.get(kind, 0)
                        column = column + (kind == "top1")
                        number = number + 1

            section(PROLOGUE, (0, 0, 0, 0), 0, 0)
            dve.wait_ge(rows_in, 32)
            section(FIRST, AT_FIRST, 1, 0)
            with dve.Fori(0, LOOPED) as t:
                section(BODY, [a + t * b for a, b in zip(AT_LOOP, IN_LOOP)], t + 2, t * HALVES + 1)
            section(LAST, AT_LAST, None, LOOPED * HALVES + 1)

        @block.tensor
        def _(pe):
            def split_product(dst, weights, values, first=True, last=True):
                terms = [(w, v) for (wh, wl), (vh, vl) in zip(weights, values)
                         for w, v in ((wh, vh), (wh, vl), (wl, vh))]
                for k, (w, v) in enumerate(terms):
                    ins = nc.tensor.matmul(dst, w, v, start=first and k == 0,
                                           stop=last and k == len(terms) - 1)
                return ins

            def turn(n, t, peeled):
                h, u = n // NU, n % NU
                if not (peeled and t == 0 and n < 2):
                    pe.wait_ge(dve_kept if n % 2 else act_kept, t * (TILE_UNITS // 2) + n // 2)
                pe.wait_ge(gathered[u], 16 * UNITS[u][1] * (HALVES * t + h + 1))
                for c in range(UNITS[u][1]):
                    last = nc.tensor.transpose(turned[n % 2][:, c, :], ring[:, UNITS[u][0] + c, :],
                                               ident[:, :])
                last.then_inc(turns, 1)

            def parts(w, k, cols_):
                return w[:, 0, k, cols_], w[:, 1, k, cols_]

            def chunk(m):
                return slice(m * P, m * P + P)

            def quarter(n, j, dst):
                half, first = j // 2, j % 2 * (MT // 2)
                outputs = slice(half * (TOP // 2), (half + 1) * (TOP // 2))
                some = range(first, first + MT // 2)
                return split_product(dst[:, half, :], [parts(z0, k, chunk(n)) for k in some],
                                     [parts(w_top1, k, outputs) for k in some],
                                     first=j % 2 == 0, last=j % 2 == 1)

            everything = slice(0, ROUND)

            def bottom1_half(r, which, dst):
                some = range(which * (M1 // 2), (which + 1) * (M1 // 2))
                for m in range(M2):
                    last = split_product(dst[:, m, :], [parts(w_bot1, k, chunk(m)) for k in some],
                                         [parts(h0[:, r % 2], k, everything) for k in some],
                                         first=which == 0, last=which == 1)
                return last

            def use(kind, n, dst):
                if kind == "bottom0":
                    start = n // 2 * ROUND
                    for c in range(2):
                        last = nc.tensor.matmul(dst[:, c, :], w_bot0[:, chunk(n % 2 * 2 + c)],
                                                dense_hlh[:, start:start + ROUND], start=True, stop=True)
                elif kind == "bottom1":
                    last = bottom1_half(n, 1, dst)
                elif kind == "bottom2":
                    last = split_product(dst[:, 0, :], [parts(w_bot2, k, chunk(0)) for k in range(M2)],
                                         [parts(h1, k, everything) for k in range(M2)])
                elif kind == "dot":
                    for g in range(8):
                        group = vecs[:, 8 * n + g, :, :]
                        last = nc.tensor.matmul(
                            dst[0:DOT_ROWS, g // 4, g % 4 * P:g % 4 * P + 4 * TABLES],
                            group.rearrange("p q f -> p (q f)")[:, 0:DOT_ROWS], group[:, :, 0:TABLES],
                            start=True, stop=True)
                elif kind == "pairs":
                    for k, a in enumerate((range(8), range(8, 13))[n]):
                        last = nc.tensor.transpose(
                            dst[:, k // 4, k % 4 * P:k % 4 * P + P],
                            dots[:, 2 * a:2 * a + 2, :].rearrange("p e g -> p (e g)"), ident[:, :])
                elif kind == "flat":
                    for b, at in enumerate((0, PAIR_PITCH - P)):
                        for q in range(4):
                            last = nc.tensor.transpose(dst[:, b, q * P:q * P + P],
                                                       pairs[:, q, at:at + P], ident[:, :])
                elif kind == "top0":
                    for c in range(2):
                        last = split_product(
                            dst[:, c, 0:TILE], [parts(w_top0, k, chunk(2 * n + c)) for k in range(4)],
                            [(x[:, 0, :], x[:, 1, :])] + [(flat_a[:, 0, e, :], flat_a[:, 1, e, :]) for e in range(2)]
                            + [(flat_b[:, 0, :], flat_b[:, 1, :])])
                elif kind == "top1":
                    last = quarter(n, 3, dst)
                last.then_inc(filled, 1)

            def section(steps, previous, before, turn_tile, peeled=False):
                order, earlier = uses(steps), uses(previous)

                def wait_processed(k):
                    a, d = ((by_act(order[:k + 1]), by_dve(order[:k + 1])) if k >= 0 else
                            (-by_act(earlier[len(earlier) + k + 1:]), -by_dve(earlier[len(earlier) + k + 1:])))
                    pe.wait_ge(act_done, before[1] + a)
                    pe.wait_ge(dve_done, before[2] + d)

                def last_of(pair, k):
                    found = [j - len(earlier) for j, s in enumerate(earlier + order[:k]) if s[2] == pair]
                    return found[-1] if found else None

                made = {}
                k = 0
                for step in steps:
                    kind, n = step[0], step[1] if len(step) > 1 else None
                    if kind == "turn":
                        turn(n, turn_tile, peeled)
                        continue
                    if kind in ("split", "zeros", "x", "x in vecs"):
                        continue
                    if kind == "half":
                        dst_pair = next(s[2] for s in order if s[:2] == ("bottom1", n))
                        layer0 = uses_named(order).index(("bottom0", 2 * n))
                        wait_processed(max(layer0, last_of(dst_pair, k) or 0))
                        if peeled and (kind, n) in RAW_NEEDED:
                            pe.wait_ge(low_made, RAW_NEEDED[kind, n])
                        bottom1_half(n, 0, banks[dst_pair])
                        continue
                    if kind == "quarter":
                        pair = next(s[2] for s in order[k:] + uses(BODY) if s[:2] == ("top1", n))
                        if step[2] == 0:
                            needs = [last_of(pair, k)]
                            if ("top0", 3) in uses_named(order[:k]):
                                needs.append(uses_named(order).index(("top0", 3)))
                            wait_processed(max(needs))
                            if peeled:
                                pe.wait_ge(low_made, RAW_NEEDED["quarter", 0])
                        quarter(n, step[2], banks[pair])
                        continue
                    if kind != "top1":
                        before_it = last_of(step[2], k) if kind != "bottom1" else None
                        operand = made.get(NEEDS.get(kind))
                        if kind == "bottom1":
                            operand = uses_named(order).index(("bottom0", 2 * n + 1))
                        needs = [j for j in (before_it, operand) if j is not None]
                        if needs:
                            wait_processed(max(needs))
                    if (kind, n) == ("dot", 0):
                        pe.wait_ge(act_kept, turn_tile * NU + (NU + 1) // 2)
                        pe.wait_ge(dve_kept, turn_tile * NU + NU // 2)
                        pe.wait_ge(x_kept, turn_tile + 1)
                        if steps is PROLOGUE:
                            pe.wait_ge(zero_made, 1)
                    if (kind, n) == ("dot", 4):
                        pe.wait_ge(act_kept, turn_tile * NU)
                        pe.wait_ge(dve_kept, turn_tile * NU)
                    if (kind, n) == ("top0", 0):
                        pe.wait_ge(x_high, turn_tile)
                        pe.wait_ge(x_low, turn_tile)
                    if peeled and (kind, n) in RAW_NEEDED:
                        pe.wait_ge(low_made, RAW_NEEDED[kind, n])
                    use(kind, n, banks[step[2]])
                    made[kind] = k
                    k += 1

            RAW_NEEDED = {("bottom0", 0): 2, ("half", 0): 3, ("bottom2", 0): 4, ("bottom0", 4): 5,
                          ("top0", 0): 9, ("quarter", 0): len(RAW)}

            pe.wait_ge(const_made, 3)
            section(PROLOGUE, [], (0, 0, 0, 0), 0, peeled=True)
            section(FIRST, PROLOGUE, AT_FIRST, 1, peeled=True)
            with pe.Fori(0, LOOPED) as t:
                section(BODY, BODY, [a + t * b for a, b in zip(AT_LOOP, IN_LOOP)], t + 2)
            section(LAST, BODY, AT_LAST, TILES)


def lay_out(inputs):
    import numpy as np

    def chunks(w):
        return np.ascontiguousarray(w.T.reshape(-1, P, w.shape[0]).transpose(1, 0, 2))

    a = {k.removeprefix("L0_rec_"): np.asarray(v) for k, v in inputs.items()}
    dense = np.zeros((PITCH, BATCH), np.float32)
    dense[0:DENSE] = a["r_dense_x"].T.reshape(DENSE, TILES, 2, 4, 32).transpose(0, 1, 3, 2, 4)\
        .reshape(DENSE, BATCH)
    dense[DENSE] = 1
    bot_w0 = np.zeros((PITCH, BOT1), np.float32)
    bot_w0[0:DENSE] = a["bot_w0"].T
    bot_w0[DENSE] = a["bot_b0"]
    w0 = a["top_w0"]
    top_w0 = np.zeros((P, 4, TOP), w0.dtype)
    top_w0[:, 0] = w0[:, 0:D].T
    for j in range(TABLES):
        for i in range(j + 1, FEATURES):
            r = START[j // 2] + i - (j // 2 * 2 + 1)
            column = w0[:, D + i * (i - 1) // 2 + j]
            if r < P:
                top_w0[r, 1 + j % 2] = column
            else:
                top_w0[r - P + 64 * (j % 2), 3] = column
    top_w0[HALF_PAIRS - P, 3] = a["top_b0"]
    columns = np.zeros((P, COLUMNS), np.float32)
    for at, v in ((COL_B1, a["bot_b1"]), (COL_B2, a["bot_b2"])):
        columns[:, at:at + v.size // P] = v.reshape(-1, P).T
    columns[:, COL_LAST] = a["top_b2"][0]
    return {
        "indices": np.ascontiguousarray(a["r_lS_i"].reshape(TABLES, -1, P).transpose(2, 1, 0)),
        "tables": np.ascontiguousarray(a["emb_W"]),
        "dense": dense,
        "bot_w0": bot_w0,
        "bot_w1": chunks(a["bot_w1"]),
        "bot_w2": chunks(a["bot_w2"]),
        "top_w0": top_w0,
        "top_w1": chunks(a["top_w1"]),
        "columns": columns,
        "top_b1": np.ascontiguousarray(a["top_b1"].reshape(1, TOP)),
        "top_w2": np.ascontiguousarray(a["top_w2"].reshape(1, TOP)),
    }


def kernel(**inputs):
    import concourse.bacc as bacc
    from concourse.bass_utils import run_bass_kernel_spmd

    nc = bacc.Bacc("TRN2", target_bir_lowering=False, num_devices=1)
    arrays = lay_out(inputs)
    args = [nc.dram_tensor(n, v.shape, mybir.dt.from_np(v.dtype), kind="ExternalInput").ap()
            for n, v in arrays.items()]
    out = nc.dram_tensor("out", (P, BATCH // P), F32, kind="ExternalOutput").ap()
    dlrm(nc, *args, out)
    r = run_bass_kernel_spmd(nc, [arrays], core_ids=[0])
    return r.results[0]["out"].reshape(2, 2, 32, TILES, 2).transpose(3, 1, 4, 0, 2).reshape(BATCH, 1)
```

```python
import concourse.bass as bass
from concourse import mybir
from contextlib import ExitStack

F32, F32R = mybir.dt.float32, mybir.dt.float32r
I32, U32 = mybir.dt.int32, mybir.dt.uint32
ACT, ALU = mybir.ActivationFunctionType, mybir.AluOpType

P = 128
BATCH, TABLES, ROWS, D = 2048, 26, 12500, 128
DENSE, BOT1, BOT2 = 13, 512, 256
TOP = 1024
TILE = 256
TILES = BATCH // TILE
HALVES = TILE // P
GROUPS = TILE // 4
PITCH = 32
FEATURES = TABLES + 1
DOT_ROWS = 3 * PITCH + FEATURES
M1, M2, MT = BOT1 // P, BOT2 // P, TOP // P
ROUND = 512
ROUNDS = BATCH // ROUND
WIDTH = [FEATURES - 1 - 2 * a for a in range(TABLES // 2)]
START = [sum(WIDTH[:a]) for a in range(TABLES // 2)]
HALF_PAIRS = sum(WIDTH)
PAIR_PITCH = 192
UNITS = [(4 * u, min(4, TABLES - 4 * u)) for u in range(7)]
NU = len(UNITS)
TILE_UNITS = HALVES * NU
COL_B1, COL_B2, COL_LAST = 0, M2, M2 + 1
COLUMNS = COL_LAST + 1
STAGED = 1024
SLOTS = 4

OTHERS = ("turn", "split", "zeros", "x in vecs", "x", "part", "half")


def parts(n, first, end):
    return [("part", n, j) for j in range(first, end)]


def bottom(r):
    layer0 = [("bottom0", 2 * r + 2, (r + 1) % 3), ("bottom0", 2 * r + 3, (r + 2) % 3)]
    if r == ROUNDS - 1:
        return [("bottom1", r, r % 3), ("turn", 2 * r), ("turn", 2 * r + 1), ("bottom2", r, r % 3)]
    return [layer0[0], ("bottom1", r, r % 3), layer0[1], ("turn", 2 * r), ("split", 5 + r), ("half", r + 1),
            ("turn", 2 * r + 1), ("bottom2", r, r % 3)]


PROLOGUE = (
    [("split", 0), ("split", 1), ("split", 2), ("bottom0", 0, 2), ("bottom0", 1, 1), ("half", 0),
     ("split", 3), ("zeros",), ("split", 4)]
    + bottom(0) + bottom(1) + bottom(2) + bottom(3)
    + [("x in vecs",), ("split", 8), ("dot", 0, 1), ("split", 9), ("dot", 1, 2), ("split", 10),
       ("dot", 2, 1), ("turn", 8), ("dot", 3, 2), ("split", 11), ("turn", 9), ("turn", 10), ("x",),
       ("turn", 11), ("turn", 12), ("turn", 13)])
BODY = (
    [("dot", 4, 0), ("dot", 5, 1), ("turn", 0), ("dot", 6, 0), ("dot", 7, 1)]
    + parts(1, 4, 5) + [("pairs", 0, 0), ("pairs", 1, 1), ("turn", 1), ("turn", 2)]
    + parts(1, 5, 6) + [("flat", 0, 0), ("x in vecs",)]
    + parts(1, 6, 7) + [("top1", 1, 2), ("turn", 3)]
    + [("top0", 0, 1), ("turn", 4), ("top0", 1, 0), ("turn", 5), ("top0", 2, 2), ("turn", 6), ("top0", 3, 1)]
    + [("dot", 0, 0), ("dot", 1, 2), ("turn", 7), ("dot", 2, 0), ("dot", 3, 2), ("x",), ("turn", 8)]
    + parts(0, 0, 4) + [("turn", 9)] + parts(0, 4, 6) + [("turn", 10)] + parts(0, 6, 7) + [("top1", 0, 1)]
    + parts(1, 0, 2) + [("turn", 11)] + parts(1, 2, 3) + [("turn", 12), ("turn", 13)] + parts(1, 3, 4))
FIRST = [("split", 12)] + sum(([s, ("split", 9 + s[1])] if s[0] == "dot" and s[1] >= 4 else [s]
                               for s in BODY if s != ("top1", 1, 2) and s not in parts(1, 4, 7)), [])
LAST = ([s for s in BODY[:BODY.index(("dot", 0, 0))] if s[0] not in ("turn", "x in vecs")]
        + parts(0, 0, 7) + [("top1", 0, 0)] + parts(1, 0, 7) + [("top1", 1, 2)])
LOOPED = TILES - 2


def uses(steps):
    return [s for s in steps if s[0] not in OTHERS]


def top1_pair(n, steps, done):
    return next(s[2] for s in uses(steps)[done:] + uses(BODY) if s[:2] == ("top1", n))


def uses_named(steps):
    return [s[:2] for s in uses(steps)]


def by_act(steps):
    return sum(s[0] != "top1" for s in uses(steps))


def by_dve(steps):
    return sum(s[0] != "bottom2" for s in uses(steps))


def first_banks(steps):
    return sum(s[0] == "part" and s[2] == 3 for s in steps)


def dve_steps(steps):
    return sum({"bottom1": 1, "top1": 2}.get(s[0], 0) for s in steps) + first_banks(steps)


def totals(sections):
    steps = sum(sections, [])
    return len(uses(steps)), by_act(steps), by_dve(steps), dve_steps(steps), first_banks(steps)


NOTHING = totals([])
AT_FIRST = totals([PROLOGUE])
AT_LOOP = totals([PROLOGUE, FIRST])
IN_LOOP = totals([BODY])
AT_LAST = tuple(a + LOOPED * b for a, b in zip(AT_LOOP, IN_LOOP))
AT_END = tuple(a + b for a, b in zip(AT_LAST, totals([LAST])))


def dlrm(nc, indices, tables, dense, bot_w0, bot_w1, bot_w2, top_w0, top_w1, columns, top_b1, top_w2, out):
    table_rows = tables.rearrange("t r d -> (t r) d")
    ctx = ExitStack()
    with ctx:
        def sb(name, shape, dt):
            return ctx.enter_context(nc.sbuf_tensor(name, shape, dt))

        def sem(name):
            return ctx.enter_context(nc.semaphore(name))

        z0_at = (nc.sbuf_base + 31) // 32 * 32
        sb("z0_region", [P, 2 * MT * TILE], F32)
        staged = nc.alloc_sbuf_tensor_at("staged", [P, SLOTS, STAGED], F32, offset=z0_at)
        z0 = nc.alloc_sbuf_tensor_at("z0", [P, 2, MT, TILE], F32R, offset=z0_at)
        w_top1_at = (nc.sbuf_base + 31) // 32 * 32
        sb("w_top1_region", [P, 2 * MT * TOP], F32)
        w_top1 = nc.alloc_sbuf_tensor_at("w_top1", [P, 2, MT, TOP], F32R, offset=w_top1_at)
        next_at = [w_top1_at]

        def early(name, shape, dt=F32R):
            at = next_at[0]
            words = 1
            for n in shape[1:]:
                words *= n
            next_at[0] += 4 * words
            return nc.alloc_sbuf_tensor_at(name, shape, dt, offset=at)

        w_bot0 = early("w_bot0", [96, BOT1])
        dense_hlh = early("dense_hlh", [96, BATCH])
        w_bot1 = early("w_bot1", [P, 2, M1, BOT2])
        w_bot2 = early("w_bot2", [P, 2, M2, D])
        h0 = early("h0", [P, 2, 2, M1, ROUND])
        h1 = early("h1", [P, 2, M2, ROUND])
        relu = early("relu", [P, 2, ROUND], F32)
        assert next_at[0] <= w_top1_at + 8 * MT * TOP

        ring = sb("ring", [P, TABLES, D], F32)
        vecs = sb("vecs", [P, GROUPS, 4, PITCH], F32)
        dots = sb("dots", [P, TABLES, GROUPS], F32)
        w_top0 = sb("w_top0", [P, 2, 4, TOP], F32R)
        x_all = sb("x_all", [P, BATCH], F32)
        x = sb("x", [P, 2, TILE], F32R)
        flat_a = sb("flat_a", [P, 2, 2, TILE], F32R)
        flat_b = sb("flat_b", [P, 2, TILE], F32R)
        pairs = sb("pairs", [P, 4, PAIR_PITCH], F32)
        hidden = sb("hidden", [P, 2, TOP // 2], F32)
        weighed = sb("weighed", [P, 2, TOP // 2], F32)
        sums = sb("sums", [P, 2], F32)
        b1_rows = sb("b1_rows", [P, 2, TOP // 2], F32)
        w2_rows = sb("w2_rows", [P, 2, TOP // 2], F32)
        logits = sb("logits", [P, BATCH // P], F32)
        probs = sb("probs", [P, BATCH // P], F32)
        rows = sb("rows", [P, (TILES + 1) * HALVES, TABLES], I32)
        row_now = [sb(f"row_now{h}", [P, TABLES], U32) for h in range(HALVES)]
        cols = sb("cols", [P, COLUMNS], F32)
        ident = sb("ident", [P, P], F32)
        wrap = hidden[:, :, :].bitcast(I32).rearrange("p a n -> p (a n)")
        base = weighed[:, :, :].bitcast(I32).rearrange("p a n -> p (a n)")

        turned = [ctx.enter_context(nc.psum_tensor(f"turned{n}", [P, 4, P], F32)) for n in range(2)]
        banks = [ctx.enter_context(nc.psum_tensor(f"banks{n}", [P, 2, 512], F32)) for n in range(3)]

        first_idx_in = sem("first_idx_in")
        idx_in, cols_in, rows_in = sem("idx_in"), sem("cols_in"), sem("rows_in")
        raw_in = [sem(f"raw_in{n}") for n in range(SLOTS)]
        high_made, low_made = sem("high_made"), sem("low_made")
        const_made = sem("const_made")
        zero_made = sem("zero_made")
        rows_step = sem("rows_step")
        row_ready = [sem(f"row_ready{h}") for h in range(HALVES)]
        gathered = [sem(f"gathered{u}") for u in range(NU)]
        turns = sem("turns")
        act_kept, dve_kept = sem("act_kept"), sem("dve_kept")
        x_kept = sem("x_kept")
        x_high, x_low = sem("x_high"), sem("x_low")
        filled = sem("filled")
        first_bank_filled = sem("first_bank_filled")
        act_done, dve_done = sem("act_done"), sem("dve_done")
        dve_step = sem("dve_step")
        probs_made, sent = sem("probs_made"), sem("sent")

        RAW = ([("bot0", 0, 96, BOT1), ("dense", 0, 96, STAGED), ("bot1", 0, P, M1 * BOT2),
                ("bot2", 0, P, M2 * D), ("dense", 1, 96, STAGED)]
               + [("top0", k, P, TOP) for k in range(4)] + [("top1", k, P, TOP) for k in range(MT)])
        RAW_DMAS = [3 if nrows == 96 else 1 for _, _, nrows, _ in RAW]

        def raw_parts(n):
            kind, k, nrows, ncols = RAW[n]
            slot = staged[0:nrows, n % SLOTS, 0:ncols]
            if kind == "bot0":
                return slot, w_bot0[:, :], None
            if kind == "dense":
                return slot, dense_hlh[:, k * STAGED:(k + 1) * STAGED], None
            if kind in ("bot1", "bot2"):
                w = w_bot1 if kind == "bot1" else w_bot2
                return slot, *(w[:, s, :, :].rearrange("p k m -> p (k m)") for s in range(2))
            w = w_top0 if kind == "top0" else w_top1
            return slot, w[:, 0, k, :], w[:, 1, k, :]

        def raw_count(n):
            return 16 * sum(RAW_DMAS[n % SLOTS:n + 1:SLOTS])

        def vecs_out(n):
            h, (first, count) = n // NU, UNITS[n % NU]
            return vecs[:, 32 * h:32 * h + 32, :, 1 + first:1 + first + count].rearrange("p g q f -> p f q g")

        def turned_in(n):
            return turned[n % 2][:, 0:UNITS[n % NU][1], :].rearrange("p f (q g) -> p f q g", q=4)

        def dots_in(src, q):
            groups = src[32 * q:32 * q + (32 if q < 3 else FEATURES), :, :].rearrange("i b (g c) -> i (b g) c", g=4)
            return groups[:, :, q * TABLES:(q + 1) * TABLES]

        def dots_out(n, q):
            return dots[32 * q:32 * q + (32 if q < 3 else FEATURES), :, 8 * n:8 * n + 8].rearrange("i j g -> i g j")

        def pairs_in(src, bank, a):
            block_ = src[:, bank, :].rearrange("p (a q i) -> p a q i", a=4, q=4)
            return block_[:, a % 4, :, 2 * a + 1:FEATURES]

        def pairs_out(a):
            return pairs[:, :, START[a]:START[a] + WIDTH[a]]

        def flat_a_in(src, parity):
            return src[:, 0, :].rearrange("p (q e g) -> p e q g", q=4, e=2)[:, parity]

        def flat_b_in(src, parity):
            return src[64:128, 1, :].rearrange("p (q e g) -> p e q g", q=4, e=2)[:, parity]

        def by_q(samples):
            return samples.rearrange("p (q g) -> p q g", q=4)

        x_in_vecs = vecs[:, :, :, 0].rearrange("p g q -> p q g")

        def x_of(tile):
            return x_all[:, bass.ds(tile * TILE, TILE)]

        def z0_use(n, part):
            return z0[:, part, 2 * n:2 * n + 2, :]

        block = ctx.enter_context(nc.Block())

        @block.sync
        def _(sp):
            for arrived, halves in ((first_idx_in, slice(0, HALVES)), (idx_in, slice(HALVES, TILES * HALVES))):
                sp.dma_start(rows[:, halves, :], indices[:, halves, :]).then_inc(arrived, 16)
            for n, (kind, k, nrows, ncols) in enumerate(RAW):
                if n >= SLOTS:
                    sp.wait_ge(low_made, n - SLOTS + 1)
                if kind in ("bot0", "dense"):
                    src = bot_w0 if kind == "bot0" else dense[:, k * STAGED:(k + 1) * STAGED]
                    for c in range(3):
                        sp.dma_start(staged[32 * c:32 * c + 32, n % SLOTS, 0:ncols], src)\
                          .then_inc(raw_in[n % SLOTS], 16)
                else:
                    src = {"bot1": bot_w1, "bot2": bot_w2}.get(kind)
                    if src is None:
                        src = (top_w0 if kind == "top0" else top_w1)[:, k, :]
                    sp.dma_start(staged[:, n % SLOTS, 0:ncols], src).then_inc(raw_in[n % SLOTS], 16)
                if n == 0:
                    sp.dma_start(cols[:, :], columns).then_inc(cols_in, 16)
                if n == 8:
                    for row, values in ((b1_rows, top_b1), (w2_rows, top_w2)):
                        sp.dma_start(row[:, :, :].rearrange("p a n -> p (a n)"),
                                     values.to_broadcast([P, TOP])).then_inc(rows_in, 16)
            sp.wait_ge(probs_made, 1)
            sp.dma_start(out, probs[:, :]).then_inc(sent, 16)
            sp.wait_ge(sent, 16)

        @block.gpsimd
        def _(pool):
            nc.gpsimd.iota(base[:, 0:TILES * HALVES * TABLES], pattern=[[0, TILES * HALVES], [ROWS, TABLES]],
                           base=0, channel_multiplier=0).then_inc(const_made, 1)
            nc.gpsimd.memset(ident[:, :], 0.0).then_inc(const_made, 1)
            pool.wait_ge(const_made, 2)
            nc.gpsimd.affine_select(out=ident[:, :], in_=ident[:, :], compare_op=ALU.not_equal, fill=1.0,
                                    base=0, pattern=[[-1, P]], channel_multiplier=1)\
              .then_inc(const_made, 1)

            def gather_unit(h, u):
                first, count = UNITS[u]
                for f in range(first, first + count):
                    nc.gpsimd.indirect_dma_start(
                        out=ring[:, f, :], out_offset=None, in_=table_rows,
                        in_offset=bass.IndirectOffsetOnAxis(ap=row_now[h][:, f:f + 1], axis=0))\
                      .then_inc(gathered[u], 16)

            pool.wait_ge(row_ready[0], 1)
            pool.wait_ge(row_ready[1], 1)
            for u in range(NU):
                gather_unit(0, u)
            for u in range(NU):
                pool.wait_ge(turns, u + 1)
                gather_unit(1, u)
            units_turned = pool.alloc_register("units_turned")
            rows_given = pool.alloc_register("rows_given")
            pool.reg_mov(units_turned, NU)
            pool.reg_mov(rows_given, 1)
            with pool.Fori(1, TILES):
                pool.reg_add(rows_given, rows_given, 1)
                for h in range(HALVES):
                    for u in range(NU):
                        pool.reg_add(units_turned, units_turned, 1)
                        pool.wait_ge(const_made, 3)
                        if u == 0:
                            pool.wait_ge(row_ready[h], rows_given)
                        pool.wait_ge(turns, units_turned)
                        gather_unit(h, u)

        @block.scalar
        def _(act):
            act.wait_ge(cols_in, 16)
            nc.scalar.activation(probs[:, 0:1], cols[:, 0:1], ACT.Sigmoid)

            def split(n):
                slot, high, _ = raw_parts(n)
                act.wait_ge(raw_in[n % SLOTS], raw_count(n))
                nc.scalar.activation(high, slot, ACT.Copy).then_inc(high_made, 1)

            def turn(n, t):
                if n % 2 == 0:
                    act.wait_ge(turns, t * TILE_UNITS + n + 1)
                    nc.scalar.activation(vecs_out(n), turned_in(n), ACT.Copy).then_inc(act_kept, 1)

            def keep_x(tile):
                nc.scalar.activation(x_in_vecs, by_q(x_of(tile)), ACT.Copy).then_inc(x_kept, 1)

            def take_x(tile):
                nc.scalar.activation(x[:, 0, :], x_of(tile), ACT.Copy).then_inc(x_high, 1)

            def use(kind, n, number, src, first):
                act.wait_ge(filled, number + 1)
                if kind == "bottom0":
                    m = n % 2 * 2
                    last = nc.scalar.activation(h0[:, n // 2 % 2, 0, m:m + 2, :], src[:, :, :], ACT.Relu)
                elif kind == "bottom1":
                    bias = cols[:, COL_B1:COL_B1 + 1]
                    nc.scalar.activation(relu[:, 0, :], src[:, 0, :], ACT.Relu, bias=bias)
                    last = nc.scalar.activation(h1[:, 0, 0, :], src[:, 0, :], ACT.Relu, bias=bias)
                elif kind == "bottom2":
                    last = nc.scalar.activation(x_all[:, n * ROUND:(n + 1) * ROUND], src[:, 0, :], ACT.Relu,
                                                bias=cols[:, COL_B2:COL_B2 + 1])
                elif kind == "dot":
                    for q in (0, 1):
                        last = nc.scalar.activation(dots_out(n, q), dots_in(src, q), ACT.Copy)
                elif kind == "pairs":
                    for a in ((0, 1, 2, 3), (8, 9, 10, 11))[n]:
                        last = nc.scalar.activation(pairs_out(a), pairs_in(src, 0, a), ACT.Copy)
                elif kind == "flat":
                    for e in range(2):
                        nc.scalar.activation(by_q(flat_a[:, 0, e, :]), flat_a_in(src, e), ACT.Copy)
                        last = nc.scalar.activation(by_q(flat_b[64 * e:64 * e + 64, 0, :]),
                                                    flat_b_in(src, e), ACT.Copy)
                elif kind == "top0":
                    if first:
                        act.wait_ge(low_made, len(RAW))
                    last = nc.scalar.activation(z0_use(n, 0), src[:, :, 0:TILE], ACT.Relu)
                last.then_inc(act_done, 1)

            def section(steps, before, turn_tile):
                number = before[0]
                for kind, *n in steps:
                    if kind == "turn":
                        turn(n[0], turn_tile)
                    elif kind == "split":
                        split(n[0])
                    elif kind == "x in vecs":
                        keep_x(turn_tile)
                    elif kind == "x":
                        take_x(turn_tile)
                    elif kind not in OTHERS:
                        if kind != "top1":
                            use(kind, n[0], number, banks[n[1]], steps is FIRST)
                        number = number + 1

            section(PROLOGUE, NOTHING, 0)
            section(FIRST, AT_FIRST, 1)
            with act.Fori(0, LOOPED) as t:
                section(BODY, [a + t * b for a, b in zip(AT_LOOP, IN_LOOP)], t + 2)
            section(LAST, AT_LAST, None)
            act.wait_ge(dve_done, AT_END[2])
            nc.scalar.activation(probs[:, :], logits[:, :], ACT.Sigmoid, bias=cols[:, COL_LAST:COL_LAST + 1])\
              .then_inc(probs_made, 1)

        @block.vector
        def _(dve):
            def make_rows(lo, hi, steps):
                part = rows[:, lo:hi, :].rearrange("p h t -> p (h t)")
                count = (hi - lo) * TABLES
                nc.vector.tensor_scalar(wrap[:, 0:count], part, 0.0, float(ROWS), ALU.is_lt, ALU.mult)\
                  .then_inc(rows_step, 1)
                dve.wait_ge(rows_step, steps + 1)
                nc.vector.tensor_tensor(part, part, wrap[:, 0:count], ALU.add).then_inc(rows_step, 1)
                dve.wait_ge(rows_step, steps + 2)
                nc.vector.tensor_scalar(part, part, 0.0, float(ROWS - 1), ALU.max, ALU.min)\
                  .then_inc(rows_step, 1)
                dve.wait_ge(rows_step, steps + 3)
                nc.vector.tensor_tensor(part, part, base[:, lo * TABLES:hi * TABLES], ALU.add)\
                  .then_inc(rows_step, 1)
                dve.wait_ge(rows_step, steps + 4)

            def give_rows(h, t):
                nc.vector.tensor_copy(row_now[h][:, :], rows[:, 2 * t + h, :].bitcast(U32))\
                  .then_inc(row_ready[h], 1)

            dve.wait_ge(first_idx_in, 16)
            dve.wait_ge(const_made, 1)
            make_rows(0, HALVES, 0)
            give_rows(0, 0)
            give_rows(1, 0)

            def zeros():
                nc.vector.memset(vecs[:, :, :, FEATURES:PITCH], 0.0)
                nc.vector.memset(dots[96:128, :, :], 0.0)
                nc.vector.memset(pairs[:, :, HALF_PAIRS:HALF_PAIRS + 1], 1.0)
                nc.vector.memset(pairs[:, :, HALF_PAIRS + 1:PAIR_PITCH], 0.0).then_inc(zero_made, 1)
                dve.wait_ge(idx_in, 16)
                make_rows(HALVES, HALVES * TILES, 4)
                nc.vector.memset(rows[:, HALVES * TILES:, :], 0)

            def split(n):
                slot, high, low = raw_parts(n)
                dve.wait_ge(high_made, n + 1)
                if RAW[n][0] == "bot0":
                    low, high, slot = high[64:96], high[64:96], slot[64:96]
                elif RAW[n][0] == "dense":
                    low, high, slot = high[32:64], high[32:64], slot[32:64]
                nc.vector.tensor_tensor(low, slot, high.bitcast(F32), ALU.subtract).then_inc(low_made, 1)

            def turn(n, t):
                if n % 2:
                    dve.wait_ge(turns, t * TILE_UNITS + n + 1)
                    nc.vector.tensor_copy(vecs_out(n), turned_in(n)).then_inc(dve_kept, 1)

            def take_x(tile):
                dve.wait_ge(x_high, tile + 1)
                nc.vector.tensor_tensor(x[:, 1, :], x_of(tile), x[:, 0, :].bitcast(F32), ALU.subtract)\
                  .then_inc(x_low, 1)

            def relu_low(low, src, high):
                return nc.vector.scalar_tensor_tensor(low, src, 0.0, high.bitcast(F32), ALU.max, ALU.subtract)

            def weigh(bank, src, steps):
                nc.vector.tensor_tensor(hidden[:, bank, :], src[:, bank, :], b1_rows[:, bank, :], ALU.add)\
                  .then_inc(dve_step, 1)
                dve.wait_ge(dve_step, steps + 1)
                return nc.vector.scalar_tensor_tensor(
                    weighed[:, bank, :], hidden[:, bank, :], 0.0, w2_rows[:, bank, :],
                    ALU.max, ALU.mult, accum_out=sums[:, bank:bank + 1])

            def use(kind, n, number, src, acts, steps, column):
                dve.wait_ge(filled, number + 1)
                if kind in ("bottom0", "flat", "top0"):
                    dve.wait_ge(act_done, acts)
                if kind == "bottom0":
                    m = n % 2 * 2
                    out0 = h0[:, n // 2 % 2, :, m:m + 2, :]
                    last = relu_low(out0[:, 1], src[:, :, :], out0[:, 0])
                elif kind == "bottom1":
                    bias = cols[:, COL_B1 + 1:COL_B1 + 2]
                    nc.vector.tensor_scalar(relu[:, 1, :], src[:, 1, :], bias, 0.0, ALU.add, ALU.max)
                    nc.vector.tensor_scalar(h1[:, 0, 1, :], src[:, 1, :], bias, 0.0, ALU.add, ALU.max)\
                      .then_inc(dve_step, 1)
                    dve.wait_ge(act_done, acts)
                    dve.wait_ge(dve_step, steps + 1)
                    last = nc.vector.tensor_tensor(h1[:, 1, :, :], relu[:, :, :],
                                                   h1[:, 0, :, :].bitcast(F32), ALU.subtract)
                elif kind == "dot":
                    for q in (2, 3):
                        last = nc.vector.tensor_copy(dots_out(n, q), dots_in(src, q))
                elif kind == "pairs":
                    for a in ((4, 5, 6, 7), (12,))[n]:
                        last = nc.vector.tensor_copy(pairs_out(a), pairs_in(src, 1, a))
                elif kind == "flat":
                    for e in range(2):
                        nc.vector.tensor_tensor(by_q(flat_a[:, 1, e, :]), flat_a_in(src, e),
                                                by_q(flat_a[:, 0, e, :].bitcast(F32)), ALU.subtract)
                        half = flat_b[64 * e:64 * e + 64]
                        last = nc.vector.tensor_tensor(by_q(half[:, 1, :]), flat_b_in(src, e),
                                                       by_q(half[:, 0, :].bitcast(F32)), ALU.subtract)
                elif kind == "top0":
                    last = relu_low(z0_use(n, 1), src[:, :, 0:TILE], z0_use(n, 0))
                elif kind == "top1":
                    weigh(1, src, steps).then_inc(dve_step, 1)
                    dve.wait_ge(dve_step, steps + 2)
                    last = nc.vector.tensor_tensor(logits[:, bass.ds(column, 1)], sums[:, 0:1],
                                                   sums[:, 1:2], ALU.add)
                last.then_inc(dve_done, 1)

            def section(steps, before, turn_tile, column):
                number, acts, _, own, first_banks_before = before
                done = 0
                for kind, *n in steps:
                    if kind == "turn":
                        turn(n[0], turn_tile)
                        if n[0] in (7, 13):
                            give_rows(0 if n[0] == 7 else 1, turn_tile + 1)
                    elif kind == "split":
                        split(n[0])
                    elif kind == "zeros":
                        zeros()
                    elif kind == "x":
                        take_x(turn_tile)
                    elif kind == "part" and n[1] == 3:
                        dve.wait_ge(first_bank_filled, first_banks_before + 1)
                        weigh(0, banks[top1_pair(n[0], steps, done)], own)
                        own = own + 1
                        first_banks_before = first_banks_before + 1
                    elif kind not in OTHERS:
                        acts = acts + (kind != "top1")
                        if kind != "bottom2":
                            use(kind, n[0], number, banks[n[1]], acts, own, column)
                        own = own + {"bottom1": 1, "top1": 2}.get(kind, 0)
                        column = column + (kind == "top1")
                        done = done + 1
                        number = number + 1

            section(PROLOGUE, NOTHING, 0, 0)
            dve.wait_ge(rows_in, 32)
            section(FIRST, AT_FIRST, 1, 0)
            with dve.Fori(0, LOOPED) as t:
                section(BODY, [a + t * b for a, b in zip(AT_LOOP, IN_LOOP)], t + 2, t * HALVES + 1)
            section(LAST, AT_LAST, None, LOOPED * HALVES + 1)

        @block.tensor
        def _(pe):
            def split_product(dst, weights, values, first=True, last=True):
                terms = [(w, v) for (wh, wl), (vh, vl) in zip(weights, values)
                         for w, v in ((wh, vh), (wh, vl), (wl, vh))]
                for k, (w, v) in enumerate(terms):
                    ins = nc.tensor.matmul(dst, w, v, start=first and k == 0,
                                           stop=last and k == len(terms) - 1)
                return ins

            def turn(n, t, peeled):
                h, u = n // NU, n % NU
                if not (peeled and t == 0 and n < 2):
                    pe.wait_ge(dve_kept if n % 2 else act_kept, t * (TILE_UNITS // 2) + n // 2)
                pe.wait_ge(gathered[u], 16 * UNITS[u][1] * (HALVES * t + h + 1))
                for c in range(UNITS[u][1]):
                    last = nc.tensor.transpose(turned[n % 2][:, c, :], ring[:, UNITS[u][0] + c, :],
                                               ident[:, :])
                last.then_inc(turns, 1)

            def parts_of(w, k, cols_):
                return w[:, 0, k, cols_], w[:, 1, k, cols_]

            def chunk(m):
                return slice(m * P, m * P + P)

            def top1_part(n, j, dst):
                half, first = j // 4, j % 4 * (MT // 4)
                outputs = slice(half * (TOP // 2), (half + 1) * (TOP // 2))
                some = range(first, first + MT // 4)
                return split_product(dst[:, half, :], [parts_of(z0, k, chunk(n)) for k in some],
                                     [parts_of(w_top1, k, outputs) for k in some],
                                     first=j % 4 == 0, last=j % 4 == 3)

            everything = slice(0, ROUND)

            def bottom1_half(r, which, dst):
                some = range(which * (M1 // 2), (which + 1) * (M1 // 2))
                for m in range(M2):
                    last = split_product(dst[:, m, :], [parts_of(w_bot1, k, chunk(m)) for k in some],
                                         [parts_of(h0[:, r % 2], k, everything) for k in some],
                                         first=which == 0, last=which == 1)
                return last

            def use(kind, n, dst):
                if kind == "bottom0":
                    start = n // 2 * ROUND
                    for c in range(2):
                        last = nc.tensor.matmul(dst[:, c, :], w_bot0[:, chunk(n % 2 * 2 + c)],
                                                dense_hlh[:, start:start + ROUND], start=True, stop=True)
                elif kind == "bottom1":
                    last = bottom1_half(n, 1, dst)
                elif kind == "bottom2":
                    last = split_product(dst[:, 0, :], [parts_of(w_bot2, k, chunk(0)) for k in range(M2)],
                                         [parts_of(h1, k, everything) for k in range(M2)])
                elif kind == "dot":
                    for g in range(8):
                        group = vecs[:, 8 * n + g, :, :]
                        last = nc.tensor.matmul(
                            dst[0:DOT_ROWS, g // 4, g % 4 * P:g % 4 * P + 4 * TABLES],
                            group.rearrange("p q f -> p (q f)")[:, 0:DOT_ROWS], group[:, :, 0:TABLES],
                            start=True, stop=True)
                elif kind == "pairs":
                    for k, a in enumerate((range(8), range(8, 13))[n]):
                        last = nc.tensor.transpose(
                            dst[:, k // 4, k % 4 * P:k % 4 * P + P],
                            dots[:, 2 * a:2 * a + 2, :].rearrange("p e g -> p (e g)"), ident[:, :])
                elif kind == "flat":
                    for b, at in enumerate((0, PAIR_PITCH - P)):
                        for q in range(4):
                            last = nc.tensor.transpose(dst[:, b, q * P:q * P + P],
                                                       pairs[:, q, at:at + P], ident[:, :])
                elif kind == "top0":
                    for c in range(2):
                        last = split_product(
                            dst[:, c, 0:TILE], [parts_of(w_top0, k, chunk(2 * n + c)) for k in range(4)],
                            [(x[:, 0, :], x[:, 1, :])] + [(flat_a[:, 0, e, :], flat_a[:, 1, e, :]) for e in range(2)]
                            + [(flat_b[:, 0, :], flat_b[:, 1, :])])
                elif kind == "top1":
                    last = top1_part(n, 7, dst)
                last.then_inc(filled, 1)

            def section(steps, previous, before, turn_tile, peeled=False):
                order, earlier = uses(steps), uses(previous)

                def wait_processed(k):
                    a, d = ((by_act(order[:k + 1]), by_dve(order[:k + 1])) if k >= 0 else
                            (-by_act(earlier[len(earlier) + k + 1:]), -by_dve(earlier[len(earlier) + k + 1:])))
                    pe.wait_ge(act_done, before[1] + a)
                    pe.wait_ge(dve_done, before[2] + d)

                def last_of(pair, k, none=None):
                    found = [j - len(earlier) for j, s in enumerate(earlier + order[:k]) if s[2] == pair]
                    return found[-1] if found else none

                def place(kind, n):
                    return uses_named(order).index((kind, n))

                k = 0
                for step in steps:
                    kind, n = step[0], step[1] if len(step) > 1 else None
                    if kind == "turn":
                        turn(n, turn_tile, peeled)
                        continue
                    if kind in ("split", "zeros", "x", "x in vecs"):
                        continue
                    if kind == "half":
                        pair = order[place("bottom1", n)][2]
                        wait_processed(max(place("bottom0", 2 * n), last_of(pair, k, -1)))
                        if n == 0:
                            pe.wait_ge(low_made, 3)
                        bottom1_half(n, 0, banks[pair])
                        continue
                    if kind == "part":
                        j, pair = step[2], top1_pair(n, steps, k)
                        if n == 0 and j == 0:
                            wait_processed(max(place("top0", 1), last_of(pair, k)))
                            if peeled:
                                pe.wait_ge(low_made, len(RAW))
                        if n == 0 and j == 2:
                            wait_processed(place("top0", 3))
                        if n == 1 and j == 0:
                            wait_processed(last_of(pair, k))
                        last = top1_part(n, j, banks[pair])
                        if j == 3:
                            last.then_inc(first_bank_filled, 1)
                        continue
                    if kind == "bottom1":
                        wait_processed(place("bottom0", 2 * n + 1))
                    elif kind == "bottom2":
                        wait_processed(max(place("bottom1", n), last_of(step[2], k)))
                    elif kind == "pairs":
                        wait_processed(max(place("dot", 7), last_of(step[2], k)))
                    elif kind == "flat":
                        wait_processed(max(place("pairs", 1), last_of(step[2], k)))
                    elif kind == "top0":
                        wait_processed(max(place("flat", 0), last_of(step[2], k)))
                    elif kind != "top1" and last_of(step[2], k) is not None:
                        wait_processed(last_of(step[2], k))
                    if (kind, n) == ("dot", 0):
                        pe.wait_ge(act_kept, turn_tile * NU + (NU + 1) // 2)
                        pe.wait_ge(dve_kept, turn_tile * NU + NU // 2)
                        pe.wait_ge(x_kept, turn_tile + 1)
                        if steps is PROLOGUE:
                            pe.wait_ge(zero_made, 1)
                    if (kind, n) == ("dot", 4):
                        pe.wait_ge(act_kept, turn_tile * NU)
                        pe.wait_ge(dve_kept, turn_tile * NU)
                    if (kind, n) == ("top0", 0):
                        pe.wait_ge(x_high, turn_tile)
                        pe.wait_ge(x_low, turn_tile)
                        if peeled:
                            pe.wait_ge(low_made, 9)
                    if (kind, n) == ("bottom0", 0):
                        pe.wait_ge(low_made, 2)
                    if (kind, n) == ("bottom0", 4):
                        pe.wait_ge(low_made, 5)
                    if (kind, n) == ("bottom2", 0):
                        pe.wait_ge(low_made, 4)
                    use(kind, n, banks[step[2]])
                    k += 1

            pe.wait_ge(const_made, 3)
            section(PROLOGUE, [], NOTHING, 0, peeled=True)
            section(FIRST, PROLOGUE, AT_FIRST, 1, peeled=True)
            with pe.Fori(0, LOOPED) as t:
                section(BODY, BODY, [a + t * b for a, b in zip(AT_LOOP, IN_LOOP)], t + 2)
            section(LAST, BODY, AT_LAST, TILES)


def lay_out(inputs):
    import numpy as np

    def chunks(w):
        return np.ascontiguousarray(w.T.reshape(-1, P, w.shape[0]).transpose(1, 0, 2))

    a = {k.removeprefix("L0_rec_"): np.asarray(v) for k, v in inputs.items()}
    dense = np.zeros((PITCH, BATCH), np.float32)
    dense[0:DENSE] = a["r_dense_x"].T.reshape(DENSE, TILES, 2, 4, 32).transpose(0, 1, 3, 2, 4)\
        .reshape(DENSE, BATCH)
    dense[DENSE] = 1
    bot_w0 = np.zeros((PITCH, BOT1), np.float32)
    bot_w0[0:DENSE] = a["bot_w0"].T
    bot_w0[DENSE] = a["bot_b0"]
    w0 = a["top_w0"]
    top_w0 = np.zeros((P, 4, TOP), w0.dtype)
    top_w0[:, 0] = w0[:, 0:D].T
    for j in range(TABLES):
        for i in range(j + 1, FEATURES):
            r = START[j // 2] + i - (j // 2 * 2 + 1)
            column = w0[:, D + i * (i - 1) // 2 + j]
            if r < P:
                top_w0[r, 1 + j % 2] = column
            else:
                top_w0[r - P + 64 * (j % 2), 3] = column
    top_w0[HALF_PAIRS - P, 3] = a["top_b0"]
    columns = np.zeros((P, COLUMNS), np.float32)
    for at, v in ((COL_B1, a["bot_b1"]), (COL_B2, a["bot_b2"])):
        columns[:, at:at + v.size // P] = v.reshape(-1, P).T
    columns[:, COL_LAST] = a["top_b2"][0]
    return {
        "indices": np.ascontiguousarray(a["r_lS_i"].reshape(TABLES, -1, P).transpose(2, 1, 0)),
        "tables": np.ascontiguousarray(a["emb_W"]),
        "dense": dense,
        "bot_w0": bot_w0,
        "bot_w1": chunks(a["bot_w1"]),
        "bot_w2": chunks(a["bot_w2"]),
        "top_w0": top_w0,
        "top_w1": chunks(a["top_w1"]),
        "columns": columns,
        "top_b1": np.ascontiguousarray(a["top_b1"].reshape(1, TOP)),
        "top_w2": np.ascontiguousarray(a["top_w2"].reshape(1, TOP)),
    }


def kernel(**inputs):
    import concourse.bacc as bacc
    from concourse.bass_utils import run_bass_kernel_spmd

    nc = bacc.Bacc("TRN2", target_bir_lowering=False, num_devices=1)
    arrays = lay_out(inputs)
    args = [nc.dram_tensor(n, v.shape, mybir.dt.from_np(v.dtype), kind="ExternalInput").ap()
            for n, v in arrays.items()]
    out = nc.dram_tensor("out", (P, BATCH // P), F32, kind="ExternalOutput").ap()
    dlrm(nc, *args, out)
    r = run_bass_kernel_spmd(nc, [arrays], core_ids=[0])
    return r.results[0]["out"].reshape(2, 2, 32, TILES, 2).transpose(3, 1, 4, 0, 2).reshape(BATCH, 1)
```
